# Optimizing a Trainium2 kernel written in Bass

```python
import numpy as np
import jax
import jax.numpy as jnp

def _softmax(x, axis=-1):
    return jax.nn.softmax(x, axis=axis)

def _gelu(x):
    return jax.nn.gelu(x, approximate=True)

def _silu(x):
    return jax.nn.silu(x)

def _sigmoid(x):
    return jax.nn.sigmoid(x)

def _layernorm(x, axis=-1, eps=1e-05):
    m = jnp.mean(x, axis=axis, keepdims=True)
    v = jnp.var(x, axis=axis, keepdims=True)
    return (x - m) / jnp.sqrt(v + eps)

def _scatter_add(tgt, idx, src, axis=0):
    return tgt.at[idx].add(src)

def _segment_sum(src, seg, n):
    return jax.ops.segment_sum(src, seg, n)
kernel_name = 'mk_prb_d1_jaxref_r8_c1bb3a'

def setup_inputs(seed: int=0):
    np.random.seed(seed)
    _w = jnp.asarray

    def _L0_attn_setup():
        import jax, jax.numpy as jnp
        import numpy as np
        N_HEADS = 16

        def _rope_tables(seq_len, head_dim, dtype=jnp.float32):
            pos = jnp.arange(seq_len, dtype=jnp.float32)[:, None]
            exps = -jnp.arange(0, head_dim, 2, dtype=jnp.float32) / head_dim
            thetas = jnp.repeat(jnp.power(10000.0, exps), 2)
            angles = pos * thetas[None, :]
            return (jnp.cos(angles).astype(dtype), jnp.sin(angles).astype(dtype))

        def _apply_rope(x, cos, sin):
            x_even = x[..., 0::2]
            x_odd = x[..., 1::2]
            x_rot = jnp.stack((-x_odd, x_even), axis=-1).reshape(x.shape)
            return x * cos[None, :, None, :] + x_rot * sin[None, :, None, :]
        key = jax.random.key(seed)
        ks = jax.random.split(key, 5)
        B, S, E = (2, 256, 256)
        scale = 1.0 / np.sqrt(E)
        return {'x': jax.random.normal(ks[0], (B, S, E), dtype=jnp.float32), 'Wq': jax.random.normal(ks[1], (E, E), dtype=jnp.float32) * scale, 'bq': jnp.zeros((E,), dtype=jnp.float32), 'Wk': jax.random.normal(ks[2], (E, E), dtype=jnp.float32) * scale, 'bk': jnp.zeros((E,), dtype=jnp.float32), 'Wv': jax.random.normal(ks[3], (E, E), dtype=jnp.float32) * scale, 'bv': jnp.zeros((E,), dtype=jnp.float32), 'Wo': jax.random.normal(ks[4], (E, E), dtype=jnp.float32) * scale, 'bo': jnp.zeros((E,), dtype=jnp.float32)}
    _L0_attn_in = _L0_attn_setup()

    def _L0_ffn_setup():
        import jax, jax.numpy as jnp
        import numpy as np
        HIDDEN = 256
        FFN = 176
        N_EXPERTS = 64
        TOP_K = 6
        N_SHARED = 2
        SHARED_FFN = FFN * N_SHARED
        ROUTED_SCALING = 1.0
        EPS = 1e-20

        def _moe_forward(x, gate_w, w_gate_up, w_down, ws_gate_up, ws_down):
            T = x.shape[0]
            logits = jnp.einsum('th,eh->te', x.astype(jnp.float32), gate_w.astype(jnp.float32))
            scores = jax.nn.softmax(logits, axis=-1)
            topk_w, topk_ids = jax.lax.top_k(scores, TOP_K)
            topk_w = topk_w / (jnp.sum(topk_w, axis=-1, keepdims=True) + EPS)
            topk_w = topk_w * ROUTED_SCALING
            comb = jnp.zeros((T, N_EXPERTS), dtype=x.dtype)
            comb = comb.at[jnp.arange(T)[:, None], topk_ids].add(topk_w.astype(x.dtype))
            gu = jnp.einsum('th,efh->tef', x, w_gate_up)
            g, u = (gu[..., :FFN], gu[..., FFN:])
            act = jax.nn.silu(g) * u
            act = act * comb[:, :, None]
            routed = jnp.einsum('tef,ehf->th', act, w_down)
            sgu = jnp.einsum('th,fh->tf', x, ws_gate_up)
            sg, su = (sgu[..., :SHARED_FFN], sgu[..., SHARED_FFN:])
            shared = jnp.einsum('tf,hf->th', jax.nn.silu(sg) * su, ws_down)
            return routed + shared
        key = jax.random.key(seed)
        k0, k1, k2, k3, k4, k5 = jax.random.split(key, 6)
        hidden_states = jax.random.normal(k0, (1, 32, HIDDEN), dtype=jnp.float32)
        gate_w = jax.random.normal(k1, (N_EXPERTS, HIDDEN), dtype=jnp.float32) * 0.05
        w_gate_up = jax.random.normal(k2, (N_EXPERTS, 2 * FFN, HIDDEN), dtype=jnp.float32) * 0.02
        w_down = jax.random.normal(k3, (N_EXPERTS, HIDDEN, FFN), dtype=jnp.float32) * 0.02
        ws_gate_up = jax.random.normal(k4, (2 * SHARED_FFN, HIDDEN), dtype=jnp.float32) * 0.02
        ws_down = jax.random.normal(k5, (HIDDEN, SHARED_FFN), dtype=jnp.float32) * 0.02
        return {'hidden_states': hidden_states, 'gate_w': gate_w, 'w_gate_up': w_gate_up, 'w_down': w_down, 'ws_gate_up': ws_gate_up, 'ws_down': ws_down}
    _L0_ffn_in = _L0_ffn_setup()
    _d = {'L0_attn_x': _L0_attn_in['x'], 'L0_attn_Wq': _L0_attn_in['Wq'], 'L0_attn_bq': _L0_attn_in['bq'], 'L0_attn_Wk': _L0_attn_in['Wk'], 'L0_attn_bk': _L0_attn_in['bk'], 'L0_attn_Wv': _L0_attn_in['Wv'], 'L0_attn_bv': _L0_attn_in['bv'], 'L0_attn_Wo': _L0_attn_in['Wo'], 'L0_attn_bo': _L0_attn_in['bo'], 'L0_ffn_gate_w': _L0_ffn_in['gate_w'], 'L0_ffn_w_gate_up': _L0_ffn_in['w_gate_up'], 'L0_ffn_w_down': _L0_ffn_in['w_down'], 'L0_ffn_ws_gate_up': _L0_ffn_in['ws_gate_up'], 'L0_ffn_ws_down': _L0_ffn_in['ws_down']}
    _x0 = _d['L0_attn_x']
    _d['L0_attn_x'] = jax.random.normal(jax.random.fold_in(jax.random.key(seed), 1), (8, 256, 256), dtype=_x0.dtype)
    del _x0
    return _d

def reference(L0_attn_x, L0_attn_Wq, L0_attn_bq, L0_attn_Wk, L0_attn_bk, L0_attn_Wv, L0_attn_bv, L0_attn_Wo, L0_attn_bo, L0_ffn_gate_w, L0_ffn_w_gate_up, L0_ffn_w_down, L0_ffn_ws_gate_up, L0_ffn_ws_down):

    def _L0_attn_ref(x, Wq, bq, Wk, bk, Wv, bv, Wo, bo):
        import jax, jax.numpy as jnp
        import numpy as np
        N_HEADS = 16

        def _rope_tables(seq_len, head_dim, dtype=jnp.float32):
            pos = jnp.arange(seq_len, dtype=jnp.float32)[:, None]
            exps = -jnp.arange(0, head_dim, 2, dtype=jnp.float32) / head_dim
            thetas = jnp.repeat(jnp.power(10000.0, exps), 2)
            angles = pos * thetas[None, :]
            return (jnp.cos(angles).astype(dtype), jnp.sin(angles).astype(dtype))

        def _apply_rope(x, cos, sin):
            x_even = x[..., 0::2]
            x_odd = x[..., 1::2]
            x_rot = jnp.stack((-x_odd, x_even), axis=-1).reshape(x.shape)
            return x * cos[None, :, None, :] + x_rot * sin[None, :, None, :]
        B, S, E = x.shape
        H = N_HEADS
        D = E // H
        cos, sin = _rope_tables(S, D, x.dtype)
        q = (x @ Wq + bq).reshape(B, S, H, D)
        k = (x @ Wk + bk).reshape(B, S, H, D)
        v = (x @ Wv + bv).reshape(B, S, H, D)
        q = _apply_rope(q, cos, sin)
        k = _apply_rope(k, cos, sin)
        scores = jnp.einsum('bshd,bthd->bhst', q, k) / jnp.sqrt(jnp.asarray(D, x.dtype))
        causal = jnp.triu(jnp.ones((S, S), dtype=bool), k=1)
        scores = jnp.where(causal[None, None], -jnp.inf, scores)
        attn = jax.nn.softmax(scores, axis=-1)
        out = jnp.einsum('bhst,bthd->bshd', attn, v).reshape(B, S, E)
        return out @ Wo + bo

    def _L0_ffn_ref(hidden_states, gate_w, w_gate_up, w_down, ws_gate_up, ws_down):
        import jax, jax.numpy as jnp
        import numpy as np
        HIDDEN = 256
        FFN = 176
        N_EXPERTS = 64
        TOP_K = 6
        N_SHARED = 2
        SHARED_FFN = FFN * N_SHARED
        ROUTED_SCALING = 1.0
        EPS = 1e-20

        def _moe_forward(x, gate_w, w_gate_up, w_down, ws_gate_up, ws_down):
            T = x.shape[0]
            logits = jnp.einsum('th,eh->te', x.astype(jnp.float32), gate_w.astype(jnp.float32))
            scores = jax.nn.softmax(logits, axis=-1)
            topk_w, topk_ids = jax.lax.top_k(scores, TOP_K)
            topk_w = topk_w / (jnp.sum(topk_w, axis=-1, keepdims=True) + EPS)
            topk_w = topk_w * ROUTED_SCALING
            comb = jnp.zeros((T, N_EXPERTS), dtype=x.dtype)
            comb = comb.at[jnp.arange(T)[:, None], topk_ids].add(topk_w.astype(x.dtype))
            gu = jnp.einsum('th,efh->tef', x, w_gate_up)
            g, u = (gu[..., :FFN], gu[..., FFN:])
            act = jax.nn.silu(g) * u
            act = act * comb[:, :, None]
            routed = jnp.einsum('tef,ehf->th', act, w_down)
            sgu = jnp.einsum('th,fh->tf', x, ws_gate_up)
            sg, su = (sgu[..., :SHARED_FFN], sgu[..., SHARED_FFN:])
            shared = jnp.einsum('tf,hf->th', jax.nn.silu(sg) * su, ws_down)
            return routed + shared
        B, S, H = hidden_states.shape
        x = hidden_states.reshape(-1, H)
        out = _moe_forward(x, gate_w, w_gate_up, w_down, ws_gate_up, ws_down)
        return out.reshape(B, S, H)
    x = L0_attn_x
    xn = _layernorm(x, axis=-1)
    x = x + _L0_attn_ref(xn, L0_attn_Wq, L0_attn_bq, L0_attn_Wk, L0_attn_bk, L0_attn_Wv, L0_attn_bv, L0_attn_Wo, L0_attn_bo) + _L0_ffn_ref(xn, L0_ffn_gate_w, L0_ffn_w_gate_up, L0_ffn_w_down, L0_ffn_ws_gate_up, L0_ffn_ws_down)
    return x

_drawn_inputs = setup_inputs


def setup_inputs(seed=0):
    import zlib

    import numpy as np

    out = dict(_drawn_inputs(seed))
    spreads = {'L0_attn_bq': (0.0, 2.0),
     'L0_attn_bk': (0.0, 2.0),
     'L0_attn_bv': (0.0, 0.61),
     'L0_attn_bo': (0.0, 0.64)}
    factors = {'L0_ffn_gate_w': 8.0,
     'L0_ffn_w_gate_up': 8.0,
     'L0_ffn_w_down': 8.0,
     'L0_ffn_ws_gate_up': 2.922,
     'L0_ffn_ws_down': 2.923}
    for name, (base, spread) in spreads.items():
        noise = np.random.default_rng([zlib.crc32(name.encode()), seed]).standard_normal(out[name].shape)
        drawn = base * np.exp(spread * noise) if base else spread * noise
        out[name] = jnp.asarray(drawn.astype(out[name].dtype))
    for name, factor in factors.items():
        out[name] = (out[name] * factor).astype(out[name].dtype)
    return out
```

```python
import concourse.bass as bass
from concourse import mybir
from contextlib import ExitStack

F32 = mybir.dt.float32
BF16 = mybir.dt.bfloat16
I32 = mybir.dt.int32
ALU = mybir.AluOpType
ACT = mybir.ActivationFunctionType
AX = mybir.AxisListType

P = 128
B, S, E, H, D = 8, 256, 256, 16, 16
T = B * S
NT = T // P
SB = S // P
EC = E // P
NE, TOPK, F = 64, 6, 176
SHARED = 2
FP = F // 2
XT = NE + SHARED
ROUTED_TILES = (T * TOPK + NE * (P - 1)) // P + 1
SHARED_TILES = SHARED * NT
TILES = SHARED_TILES + ROUTED_TILES
HP = 32
G = 4
NG = H // G
UNITS = SB * NG
QK = 2 * H * D
LN_EPS = 1e-5
TOP_EPS = 1e-20
MASKED = -1e30
XB = 4
WB = 4


def build(nc, x, wqkv, bqk, bv, bo, wo, wr, wgu, wdn, rope, tri, ident, mask, before, upto, tileno, thr, tok,
          out):
    assert ROUTED_TILES == 160 and TILES % XB == 0 and NT % 2 == 0
    xn_rows = nc.dram_tensor("xn_rows", (T, E), F32, kind="Internal").ap()
    slot_token = nc.dram_tensor("slot_token", (ROUTED_TILES * P, 1), F32, kind="Internal").ap()
    y_rows = nc.dram_tensor("y_rows", (TILES * P, E), F32, kind="Internal").ap()

    ctx = ExitStack()
    with ctx:
        def sb(name, shape, dt=F32):
            return ctx.enter_context(nc.sbuf_tensor(name, shape, dt))

        def sem(name):
            return ctx.enter_context(nc.semaphore(name))

        wqkv_sb = sb("wqkv_sb", [P, EC, 3 * E])
        wr_sb = sb("wr_sb", [P, EC, NE])
        wo_sb = sb("wo_sb", [P, EC, E])
        bqk_sb = sb("bqk_sb", [P, QK])
        bv_sb = sb("bv_sb", [P, E])
        bo_sb = sb("bo_sb", [P, E])
        rope_sb = sb("rope_sb", [P, SB, 2, 2, D])
        tri_f = sb("tri_f", [P, P])
        tri_b = sb("tri_b", [P, P], BF16)
        ones_b = sb("ones_b", [P, P], BF16)
        id_f = sb("id_f", [P, P])
        id_b = sb("id_b", [P, P], BF16)
        mask_f = sb("mask_f", [P, P])
        mask_b = sb("mask_b", [P, P], BF16)
        before_sb = sb("before_sb", [NE, NE])
        upto_sb = sb("upto_sb", [NE, NE])
        tileno_sb = sb("tileno_sb", [NE, ROUTED_TILES])
        thr_sb = sb("thr_sb", [NE, NT])
        tok_sb = sb("tok_sb", [P, NT])
        kT = sb("kT", [P, 2, NG, G, S])
        spare = kT[:, 1].rearrange("p g h s -> p (g h s)")
        qkb = spare[:, 0:2 * QK].rearrange("p (u n) -> p u n", u=2)
        rot = spare[:, 2 * QK:4 * QK].rearrange("p (u n) -> p u n", u=2)
        x_all = sb("x_all", [P, NT, E])
        stats = sb("stats", [P, NT, 6])
        mv = sb("mv", [P, NT, 2])
        var = sb("var", [P, NT])
        rstd = sb("rstd", [P, NT])
        newton = sb("newton", [P, NT])
        xn = sb("xn", [P, 2, E])
        xnT = sb("xnT", [P, 2, EC, P])
        qk_all = sb("qk_all", [P, NT, QK])
        v_all = sb("v_all", [P, NT, E])
        prob, sel, comb, key = (kT[:, 0].rearrange("p g h s -> p (g h s)")[:, i * NT * NE:(i + 1) * NT * NE]
                                .rearrange("p (t e) -> p t e", e=NE) for i in range(4))
        tmp = sb("tmp", [P, NT, NE])
        sel_b = sb("sel_b", [P, NT, NE], BF16)
        run_b = sb("run_b", [P, NT + 1, NE], BF16)
        col = sb("col", [P, NT])
        top = sb("top", [P, NT, 8])
        wsum = sb("wsum", [P, NT])
        place = sb("place", [P, NE])
        slot_f = sb("slot_f", [P, NT, 8])
        slot_i = sb("slot_i", [P, NT, 8], I32)
        slot_r = sb("slot_r", [P, NT, 8], I32)
        w6 = sb("w6", [P, NT, 8])
        cnt = sb("cnt", [NE, 1])
        over = sb("over", [NE, NT])
        ntile = sb("ntile", [NE, 1])
        ntile_b = sb("ntile_b", [NE, P])
        cend = sb("cend", [NE, 1])
        passed = sb("passed", [NE, ROUTED_TILES])
        ones_c = sb("ones_c", [NE, 1])
        tile_e = sb("tile_e", [1, TILES], I32)
        tile_ef = sb("tile_ef", [1, TILES])
        last_t = sb("last_t", [1, XT], I32)
        last_tf = sb("last_tf", [1, XT])
        zero = sb("zero", [P, ROUTED_TILES])
        stok = sb("stok", [ROUTED_TILES // 2, 2, P])
        idx_all = sb("idx_all", [P, TILES], I32)
        qkp = sb("qkp", [P, 2, SB, 2, H, HP])
        qT = sb("qT", [P, 2, NG, S])
        negm = sb("negm", [P, 2, G])
        prb = sb("prb", [P, 2, G, S])
        rsum = sb("rsum", [P, 2, H])
        rrec = sb("rrec", [P, 2, H])
        pT = sb("pT", [P, 2, G * SB, P])
        on = sb("on", [P, 2, E])
        oT = sb("oT", [P, 2, EC, P])
        wgu_sb = sb("wgu_sb", [P, WB, EC, 2 * F])
        wdn_sb = sb("wdn_sb", [FP, WB, 2, E])
        idx = sb("idx", [P, XB], I32)
        xgT = sb("xgT", [P, 2, EC, P])
        sg = sb("sg", [P, 2, F])
        hid = sb("hid", [P, 2, F])
        hT = sb("hT", [FP, 2, 2, P])
        late = qk_all[:].rearrange("p t d -> p (t d)")
        y = late[:, 0:XB * E].rearrange("p (b e) -> p b e", b=XB)
        sidx = sb("sidx", [P, TOPK], I32)
        stk = sb("stk", [P, 1])
        cidx = sb("cidx", [P, 2, TOPK], I32)
        rows_at = XB * E
        yg = late[:, rows_at:rows_at + 2 * TOPK * E].rearrange("p (u k e) -> p u k e", u=2, k=TOPK)
        rows_at += 2 * TOPK * E
        ysh = late[:, rows_at:rows_at + 2 * SHARED * E].rearrange("p (u k e) -> p u k e", u=2, k=SHARED)
        rows_at += 2 * SHARED * E
        xg = late[:, rows_at + 2 * E:rows_at + (2 + XB) * E].rearrange("p (b e) -> p b e", b=XB)
        acc = late[:, rows_at:rows_at + 2 * E].rearrange("p (u e) -> p u e", u=2)

        bank = [ctx.enter_context(nc.psum_tensor(f"bank{i}", [P, 512], F32)) for i in range(4)]
        pair = [ctx.enter_context(nc.psum_tensor(f"pair{i}", [P, 1024], F32)) for i in range(2)]

        x_in = [sem(f"x_in{i}") for i in range(4)]
        w_in = sem("w_in")
        c_in = sem("c_in")
        c_in_act = sem("c_in_act")
        var_ok = sem("var_ok"); root_ok = sem("root_ok"); drope = sem("drope"); v_ok = sem("v_ok"); drec = sem("drec"); dcomb = sem("dcomb")
        sidx_ok = sem("sidx_ok"); po_turn = sem("po_turn"); ones_ok = sem("ones_ok"); kT_clear = sem("kT_clear")
        zero_ok = sem("zero_ok")
        tab_clear = sem("tab_clear")
        consts_b = sem("consts_b")
        dchain = sem("dchain")
        ln_ok = sem("ln_ok"); xt_ok = sem("xt_ok"); xnT_ok = sem("xnT_ok"); proj_ok = sem("proj_ok")
        qkv_taken = sem("qkv_taken"); logit_ok = sem("logit_ok"); resid_ok = sem("resid_ok")
        xn_out = [sem("xn_out0"), sem("xn_out1")]
        exp_in = sem("exp_in"); exp_ok = sem("exp_ok"); chosen = sem("chosen"); ranked = sem("ranked")
        counted = sem("counted"); tiled = sem("tiled"); placed = sem("placed"); ended = sem("ended")
        passed_ok = sem("passed_ok"); plan_ok = sem("plan_ok"); slots_ok = sem("slots_ok")
        scattered = sem("scattered"); stok_in = sem("stok_in"); stokT = sem("stokT"); idx_ok = sem("idx_ok")
        tables_ok = sem("tables_ok"); weights_ok = sem("weights_ok")
        pad_ok = sem("pad_ok"); qkp_ok = sem("qkp_ok"); tq_ok = sem("tq_ok"); tq_taken = sem("tq_taken")
        s_ok = sem("s_ok"); max_ok = sem("max_ok"); exp_done = sem("exp_done"); pt_ok = sem("pt_ok")
        pt_taken = sem("pt_taken"); av_ok = sem("av_ok"); on_ok = sem("on_ok"); ot_ok = sem("ot_ok")
        ot_taken = sem("ot_taken"); wo_ok = sem("wo_ok"); res_ok = sem("res_ok")
        w_free_seen = [sem(f"w_load{i}") for i in range(WB)]
        w_ready = sem("w_ready")
        idx_col = sem("idx_col")
        xg_in = [sem(f"xg_in{i}") for i in range(XB)]
        xt_done = sem("xt_done"); xgT_ok = sem("xgT_ok"); gu_ok = sem("gu_ok"); silu_ok = sem("silu_ok")
        hid_ok = sem("hid_ok"); at_ok = sem("at_ok"); hT_ok = sem("hT_ok"); dn_ok = sem("dn_ok")
        y_ok = sem("y_ok"); y_out = [sem(f"y_out{i}") for i in range(XB)]
        cidx_ok = sem("cidx_ok"); yg_in = [sem("yg_in0"), sem("yg_in1")]
        ysh_in = [sem("ysh_in0"), sem("ysh_in1")]
        acc_ok = sem("acc_ok"); out_done = [sem("out_done0"), sem("out_done1")]

        def bc_tab(s, cs, part):
            t = rope_sb[:, s, cs, :, part::2] if part is not None else rope_sb[:, s, cs, :, :]
            n = t.shape[-1]
            return t.unsqueeze(2).to_broadcast([P, 2, H, n])

        def attention(eng, step):
            for n in range(2 * UNITS):
                step(0, n, n < UNITS, False)
            with eng.Fori(2, B - 2, 2) as b:
                for n in range(2 * UNITS):
                    step(b, n, False, False)
            for n in range(2 * UNITS):
                step(B - 2, n, False, n >= UNITS)

        def experts(stages, eng):
            def turn(i, u):
                for lead, do in stages:
                    if not isinstance(i, int) or 0 <= i + lead < TILES:
                        do(i + lead, (u + lead) % XB)

            for i in range(-max(lead for lead, _ in stages), XB):
                turn(i, i % XB)
            with eng.Fori(1, TILES // XB - 1) as j:
                for u in range(XB):
                    turn(XB * j + u, u)
            for i in range(TILES - XB, TILES):
                turn(i, i % XB)

        block = ctx.enter_context(nc.Block())

        @block.sync
        def _(sp):
            xv = x.rearrange("(t p) e -> p t e", p=P)
            q4 = NT // 4
            sp.dma_start(x_all[:, 0:q4], xv[:, 0:q4]).then_inc(x_in[0], 16)
            sp.dma_start(wqkv_sb[:], wqkv.rearrange("(c p) n -> p c n", p=P)).then_inc(w_in, 16)
            sp.dma_start(wr_sb[:], wr.rearrange("(c p) n -> p c n", p=P)).then_inc(w_in, 16)
            for i in range(1, 4):
                sp.dma_start(x_all[:, q4 * i:q4 * (i + 1)], xv[:, q4 * i:q4 * (i + 1)]).then_inc(x_in[i], 16)
            sp.dma_start(wo_sb[:], wo.rearrange("(c p) n -> p c n", p=P)).then_inc(c_in, 16)
            for dst, src in ((before_sb, before), (upto_sb, upto), (tileno_sb, tileno), (thr_sb, thr)):
                sp.dma_start(dst[:], src).then_inc(c_in, 16)
            sp.wait_ge(zero_ok, 1)
            sp.dma_start(slot_token.rearrange("(p n) o -> p (n o)", p=P), zero[:]).then_inc(tab_clear, 16)
            with sp.Fori(0, NT // 2) as j:
                for u in range(2):
                    sp.wait_ge(ln_ok, 2 * j + u + 1)
                    sp.dma_start(xn_rows[bass.ds((2 * j + u) * P, P), :], xn[:, u]).then_inc(xn_out[u], 16)
            sp.wait_ge(scattered, 16 * NT * TOPK)
            sp.dma_start(stok[:], slot_token.rearrange("(c t p) o -> t c (p o)", c=2, p=P)).then_inc(stok_in, 16)
            sp.wait_ge(tables_ok, 1)

            def load(e, s):
                sp.dma_start(wgu_sb[:, s], wgu[bass.ds(e, 1), :, :].rearrange("o p n -> p (o n)")
                             if not isinstance(e, int) else wgu[e]).then_inc(w_free_seen[s], 16)
                sp.dma_start(wdn_sb[:, s], wdn[bass.ds(e, 1), :, :].rearrange("o p n -> p (o n)")
                             if not isinstance(e, int) else wdn[e]).then_inc(w_free_seen[s], 16)

            for e in range(WB):
                load(e, e)
            for e in range(WB - 1):
                sp.wait_ge(w_free_seen[e], 32)
                sp.sem_inc(w_ready, 1)
            rounds = (XT - WB) // WB
            with sp.Fori(1, rounds + 1) as j:
                for s in range(WB):
                    sp.wait_ge(w_free_seen[(s - 1) % WB], 32 * (j + (1 if s else 0)))
                    sp.sem_inc(w_ready, 1)
                    end = sp.value_load(last_t[0:1, bass.ds(WB * (j - 1) + s, 1)], min_val=1, max_val=TILES)
                    sp.wait_ge(dn_ok, end)
                    load(WB * j + s, s)
            for e in range(WB * (rounds + 1), XT + 1):
                sp.wait_ge(w_free_seen[(e - 1) % WB], 32 * ((e - 1) // WB + 1))
                sp.sem_inc(w_ready, 1)
                if e < XT:
                    end = sp.value_load(last_t[0:1, e - WB:e - WB + 1], min_val=1, max_val=TILES)
                    sp.wait_ge(dn_ok, end)
                    load(e, e % WB)
            for s in range(XB):
                sp.wait_ge(y_out[s], 16 * (TILES // XB))

            def shared_rows(t, u):
                for s in range(SHARED):
                    sp.dma_start(ysh[:, u, s], y_rows[bass.ds((s * NT + t) * P, P), :]).then_inc(ysh_in[u], 16)

            for u in range(2):
                shared_rows(u, u)
            with sp.Fori(0, NT // 2 - 1) as j:
                for u in range(2):
                    sp.wait_ge(acc_ok, 2 * j + u + 1)
                    sp.dma_start(out[bass.ds((2 * j + u) * P, P), :], acc[:, u]).then_inc(out_done[u], 16)
                    shared_rows(2 * j + u + 2, u)
            for t in range(NT - 2, NT):
                sp.wait_ge(acc_ok, t + 1)
                sp.dma_start(out[t * P:(t + 1) * P, :], acc[:, t % 2]).then_inc(out_done[t % 2], 16)
            for u in range(2):
                sp.wait_ge(out_done[u], 16 * (NT // 2))
                sp.wait_ge(xn_out[u], 16 * (NT // 2))

        @block.gpsimd
        def _(po):
            po.memset(zero[:], 0.0).then_inc(zero_ok, 1)
            po.memset(ones_b[:], 1.0)
            po.memset(ones_c[:], 1.0).then_inc(ones_ok, 1)
            po.memset(qkp[:], 0.0).then_inc(pad_ok, 1)
            po.wait_ge(c_in_act, 16 * 8)
            with po.Fori(0, NT // 2) as j:
                for u in range(2):
                    t = 2 * j + u
                    po.wait_ge(ln_ok, t + 1)
                    po.tensor_tensor(x_all[:, bass.ds(t, 1), :], x_all[:, bass.ds(t, 1), :],
                                     bo_sb[:].unsqueeze(1), ALU.add).then_inc(resid_ok, 1)
            po.wait_ge(pad_ok, 1)
            po.wait_ge(qkv_taken, NT)
            po.memset(kT[:, 1], 0.0).then_inc(kT_clear, 1)

            def pads(b, u):
                for s in range(SB):
                    po.tensor_copy(qkp[:, u, s, :, :, 0:D].rearrange("p a h d -> p (a h) d"),
                                   qk_all[:, bass.ds(SB * b + s, 1), :].rearrange("p o (h d) -> p (o h) d", d=D)
                                   ).then_inc(qkp_ok, 1)

            po.wait_ge(qkv_taken, NT)
            for b in range(2):
                pads(b, b)
            po.wait_ge(idx_ok, 1)
            po.memset(kT[:, 0], 0.0).then_inc(kT_clear, 1)
            po.wait_ge(slots_ok, 1)
            po.wait_ge(tab_clear, 16)

            def scatter(t):
                po.tensor_copy(sidx[:, :], slot_r[:, bass.ds(t, 1), 0:TOPK]
                               .rearrange("p o k -> p (o k)")).then_inc(sidx_ok, 1)
                po.tensor_copy(stk[:, :], tok_sb[:, bass.ds(t, 1)]).then_inc(sidx_ok, 1)
                po.wait_ge(sidx_ok, 2 * t + 2)
                po.sem_inc(po_turn, 1)
                for k in range(TOPK):
                    po.indirect_dma_start(slot_token[:, :], bass.IndirectOffsetOnAxis(sidx[:, k:k + 1], 0),
                                          stk[:, :], None).then_inc(scattered, 16)
                po.wait_ge(scattered, 16 * TOPK * (t + 1))

            with po.Fori(1, B // 2) as j:
                for u in range(2):
                    for v in range(2):
                        scatter(4 * (j - 1) + 2 * u + v)
                    po.wait_ge(tq_ok, 4 * (2 * j + u) - 4)
                    pads(2 * j + u, u)
            for t in range(NT - 4, NT):
                scatter(t)
            po.wait_ge(idx_ok, 2)
            for u in range(2):
                po.wait_ge(xn_out[u], 16 * (NT // 2))

            def gather(i, u):
                po.tensor_copy(idx[:, u:u + 1], idx_all[:, bass.ds(i, 1)]).then_inc(idx_col, 1)
                po.wait_ge(idx_col, i + 1)
                po.sem_inc(po_turn, 1)
                po.indirect_dma_start(xg[:, u, :], None, xn_rows[:, :],
                                      bass.IndirectOffsetOnAxis(idx[:, u:u + 1], 0)).then_inc(xg_in[u], 16)

            po.wait_ge(qkp_ok, SB * B)
            for i in range(XB):
                gather(i, i)
            with po.Fori(1, TILES // XB) as j:
                for u in range(XB):
                    po.wait_ge(xt_done, XB * (j - 1) + u + 1)
                    gather(XB * j + u, u)
            for s in range(XB):
                po.wait_ge(y_out[s], 16 * (TILES // XB))

            def rows(t, u):
                po.tensor_copy(cidx[:, u, :], slot_i[:, bass.ds(t, 1), 0:TOPK].rearrange("p o k -> p (o k)")
                               ).then_inc(cidx_ok, 1)
                po.wait_ge(cidx_ok, t + 1)
                po.sem_inc(po_turn, 1)
                for k in range(TOPK):
                    po.indirect_dma_start(yg[:, u, k, :], None, y_rows[:, :],
                                          bass.IndirectOffsetOnAxis(cidx[:, u, k:k + 1], 0)).then_inc(yg_in[u], 16)

            for u in range(2):
                rows(u, u)
            with po.Fori(1, NT // 2) as j:
                for u in range(2):
                    po.wait_ge(acc_ok, 2 * (j - 1) + u + 1)
                    rows(2 * j + u, u)

        @block.scalar
        def _(act):
            act.dma_start(id_f[:], ident).then_inc(c_in_act, 16)
            act.dma_start(bqk_sb[:], bqk.to_broadcast([P, QK])).then_inc(c_in_act, 16)
            act.dma_start(bv_sb[:], bv.to_broadcast([P, E])).then_inc(c_in_act, 16)
            act.dma_start(bo_sb[:], bo.to_broadcast([P, E])).then_inc(c_in_act, 16)
            act.dma_start(rope_sb[:], rope).then_inc(c_in_act, 16)
            act.dma_start(tri_f[:], tri).then_inc(c_in_act, 16)
            act.dma_start(mask_f[:], mask).then_inc(c_in_act, 16)
            act.dma_start(tok_sb[:], tok).then_inc(c_in_act, 16)
            act.wait_ge(var_ok, 1)
            act.activation(rstd[:], var[:], ACT.Sqrt).then_inc(root_ok, 1)
            def xnT_copy(t, u, first=False):
                act.wait_ge(xt_ok, t + 1)
                act.activation(xnT[:, u], bank[u][:, 0:E].rearrange("p (c t) -> p c t", c=EC),
                               ACT.Copy).then_inc(xnT_ok, 1)

            def logits(t, u):
                act.wait_ge(proj_ok, t + 1)
                act.activation(prob[:, bass.ds(t, 1), :].rearrange("p o e -> p (o e)"),
                               bank[2 + u][:, 0:NE], ACT.Copy).then_inc(logit_ok, 1)

            xnT_copy(0, 0)
            with act.Fori(0, NT // 2 - 1) as j:
                for u in range(2):
                    xnT_copy(2 * j + u + 1, 1 - u)
                    logits(2 * j + u, u)
            xnT_copy(NT - 1, 1)
            logits(NT - 2, 0)
            logits(NT - 1, 1)
            act.wait_ge(exp_in, 1)
            act.activation(prob[:], prob[:], ACT.Exp).then_inc(exp_ok, 1)

            def tq_copy(b, u, r):
                s, qk = r // 2, r % 2
                act.wait_ge(tq_ok, 4 * b + r + 1)
                src = bank[r % 2][:].rearrange("p (g t) -> p g t", g=NG)
                if not qk:
                    last = act.activation(qT[:, u, :, s * P:(s + 1) * P], src, ACT.Copy)
                for h in range(G if qk else 0):
                    own = slice(h * HP, (h + 1) * HP)
                    last = act.activation(kT[own, u, :, h, s * P:(s + 1) * P], src[own], ACT.Copy)
                last.then_inc(tq_taken, 1)

            def exps(m, n, first):
                p, qt, g = n % 2, n // NG, n % NG
                act.wait_ge(max_ok, m + 1)
                if not first:
                    act.wait_ge(pt_ok, 2 * (m - 1))
                for h in range(G):
                    last = act.activation(prb[:, p, h, 0:(qt + 1) * P],
                                          pair[p][:, h * S:h * S + (qt + 1) * P], ACT.Exp,
                                          bias=negm[:, p, h:h + 1], accum_out=rsum[:, qt, g * G + h:g * G + h + 1])
                last.then_inc(exp_done, 1)

            def oT_copy(c, qt):
                act.wait_ge(ot_ok, c + 1)
                act.activation(oT[:, qt], bank[2 + qt][:, E:2 * E].rearrange("p (c t) -> p c t", c=EC),
                               ACT.Copy).then_inc(ot_taken, 1)

            def a_step(b, n, first, last_b):
                u = n // UNITS
                m, n = UNITS * b + n, n % UNITS
                if not (last_b and n == UNITS - 1):
                    exps(m + 1, (n + 1) % UNITS, first and n == 0)
                if 2 <= n < 6 and not last_b:
                    tq_copy(b + u + 1, 1 - u, n - 2)
                if n % NG == 2 and not (first and n == 2):
                    oT_copy(SB * (b + u) + (0 if n == 6 else -1), 0 if n == 6 else 1)

            act.wait_ge(kT_clear, 2)
            for r in range(4):
                tq_copy(0, 0, r)
            exps(0, 0, True)
            attention(act, a_step)
            oT_copy(SB * B - 1, 1)

            def xgT_copy(i, u):
                act.wait_ge(xt_done, i + 1)
                if not (isinstance(i, int) and i < 2):
                    act.wait_ge(gu_ok, i - 1)
                act.activation(xgT[:, u % 2], bank[u % 2][:, 0:E].rearrange("p (c t) -> p c t", c=EC),
                               ACT.Copy).then_inc(xgT_ok, 1)

            def silu(i, u):
                act.wait_ge(gu_ok, i + 1)
                if not (isinstance(i, int) and i < 2):
                    act.wait_ge(hid_ok, i - 1)
                act.activation(sg[:, u % 2], pair[u % 2][:, 0:F], ACT.Silu).then_inc(silu_ok, 1)

            def y_copy(i, u):
                act.wait_ge(dn_ok, i + 1)
                if isinstance(i, int) and i < XB:
                    pass
                else:
                    act.wait_ge(y_out[u], 16 * (i // XB) if isinstance(i, int) else (i - u) * 4)
                act.activation(y[:, u], pair[u % 2][:, 512:512 + E], ACT.Copy).then_inc(y_ok, 1)
                act.wait_ge(y_ok, i + 1)
                act.dma_start(y_rows[bass.ds(i * P, P), :], y[:, u]).then_inc(y_out[u], 16)

            experts([(3, xgT_copy), (2, silu), (0, y_copy)], act)

        @block.vector
        def _(dve):
            links = [0]

            def link(i):
                links[0] += 1
                i.then_inc(dchain, 1)
                dve.wait_ge(dchain, links[0])

            dve.wait_ge(c_in_act, 16 * 8)
            dve.tensor_copy(id_b[:], id_f[:])
            dve.tensor_copy(tri_b[:], tri_f[:])
            dve.tensor_copy(mask_b[:], mask_f[:])
            dve.memset(run_b[:, 0], 0.0).then_inc(consts_b, 1)
            def layernorm(t, u, stored):
                if not (isinstance(t, int) and t < 2):
                    dve.wait_ge(xt_ok, t - 1)
                    dve.wait_ge(xn_out[u], stored)
                dve.tensor_scalar(xn[:, u], x_all[:, bass.ds(t, 1), :].rearrange("p o e -> p (o e)"),
                                  mv[:, bass.ds(t, 1), 0:1].rearrange("p o k -> p (o k)"),
                                  rstd[:, bass.ds(t, 1)], ALU.subtract, ALU.mult).then_inc(ln_ok, 1)

            RK = 3

            def rope_tile(t, u):
                dve.wait_ge(proj_ok, t + 1)
                dve.tensor_tensor(qkb[:, u], pair[u][:, 0:QK], bqk_sb[:], ALU.add).then_inc(drope, 1)
                dve.tensor_tensor(v_all[:, bass.ds(t, 1), :].rearrange("p o e -> p (o e)"),
                                  pair[u][:, 512:512 + E], bv_sb[:], ALU.add).then_inc(v_ok, 1)
                dve.wait_ge(drope, RK * t + 1)
                q4 = qkb[:, u].rearrange("p (a h d) -> p a h d", a=2, h=H)
                r4 = rot[:, u].rearrange("p (a h d) -> p a h d", a=2, h=H)
                dve.tensor_tensor(r4[:, :, :, 0::2], q4[:, :, :, 1::2], bc_tab(u, 1, 0), ALU.mult)
                dve.tensor_tensor(r4[:, :, :, 1::2], q4[:, :, :, 0::2], bc_tab(u, 1, 1), ALU.mult).then_inc(drope, 1)
                dve.wait_ge(drope, RK * t + 2)
                dve.tensor_tensor(q4, q4, bc_tab(u, 0, None), ALU.mult).then_inc(drope, 1)
                dve.wait_ge(drope, RK * t + 3)
                dve.tensor_tensor(qk_all[:, bass.ds(t, 1), :].rearrange("p o e -> p (o e)"), qkb[:, u], rot[:, u],
                                  ALU.add).then_inc(qkv_taken, 1)

            for t in range(NT):
                dve.wait_ge(x_in[t // (NT // 4)], 16)
                last = dve.bn_stats(stats[:, t], x_all[:, t])
            link(last)
            for t in range(NT):
                last = dve.bn_aggr(mv[:, t], stats[:, t])
            link(last)
            link(dve.tensor_scalar_add(var[:], mv[:, :, 1], LN_EPS))
            dve.sem_inc(var_ok, 1)
            dve.wait_ge(root_ok, 1)
            link(dve.reciprocal(rstd[:], rstd[:]))
            link(dve.tensor_tensor(newton[:], rstd[:], rstd[:], ALU.mult))
            link(dve.tensor_tensor(newton[:], newton[:], var[:], ALU.mult))
            link(dve.tensor_scalar(newton[:], newton[:], -0.5, 1.5, ALU.mult, ALU.add))
            link(dve.tensor_tensor(rstd[:], rstd[:], newton[:], ALU.mult))
            layernorm(0, 0, None)
            layernorm(1, 1, None)
            with dve.Fori(0, NT // 2 - 1) as j:
                for u in range(2):
                    layernorm(2 * j + u + 2, u, 16 * (j + 1))
                    rope_tile(2 * j + u, u)
            for t in range(NT - 2, NT):
                rope_tile(t, t % 2)

            def over_e(a):
                return a.unsqueeze(2).to_broadcast([P, NT, NE])

            def over_t(a):
                return a.unsqueeze(1).to_broadcast([P, NT, NE])

            dve.wait_ge(logit_ok, NT)
            link(dve.tensor_reduce(col[:], prob[:], AX.X, ALU.max, negate=True))
            dve.tensor_tensor(prob[:], prob[:], over_e(col[:]), ALU.add).then_inc(exp_in, 1)
            dve.wait_ge(exp_ok, 1)
            link(dve.tensor_reduce(col[:], prob[:], AX.X, ALU.add))
            link(dve.reciprocal(col[:], col[:]))
            link(dve.tensor_tensor(prob[:], prob[:], over_e(col[:]), ALU.mult))
            for t in range(NT):
                last = dve.max(top[:, t], prob[:, t])
            link(last)
            link(dve.tensor_reduce(wsum[:], top[:, :, 0:TOPK], AX.X, ALU.add))
            link(dve.tensor_scalar_add(wsum[:], wsum[:], TOP_EPS))
            link(dve.reciprocal(wsum[:], wsum[:]))
            sixth = over_e(top[:, :, TOPK - 1])
            link(dve.tensor_tensor(sel[:], prob[:], sixth, ALU.is_gt))
            link(dve.tensor_reduce(col[:], sel[:], AX.X, ALU.add))
            link(dve.tensor_scalar(col[:], col[:], -1.0, float(TOPK), ALU.mult, ALU.add))
            link(dve.tensor_tensor(tmp[:], prob[:], sixth, ALU.is_equal))
            for t in range(NT):
                last = dve.tensor_tensor_scan(key[:, t], tmp[:, t], tmp[:, t], 0.0, ALU.add, ALU.max)
            link(last)
            link(dve.tensor_tensor(key[:], key[:], over_e(col[:]), ALU.is_le))
            link(dve.tensor_tensor(key[:], key[:], tmp[:], ALU.mult))
            link(dve.tensor_tensor(sel[:], sel[:], key[:], ALU.add))
            link(dve.tensor_tensor(comb[:], prob[:], sel[:], ALU.mult))
            link(dve.tensor_tensor(comb[:], comb[:], over_e(wsum[:]), ALU.mult))
            link(dve.tensor_copy(sel_b[:], sel[:]))
            for t in range(NT):
                link(dve.tensor_tensor(run_b[:, t + 1], run_b[:, t], sel_b[:, t], ALU.add))
            dve.sem_inc(chosen, 1)
            dve.wait_ge(counted, 1)
            link(dve.tensor_copy(cnt[:], bank[2][0:NE, 0:1]))
            dve.wait_ge(c_in, 16 * 5)
            link(dve.tensor_scalar(over[:], thr_sb[:], cnt[:], None, ALU.is_lt))
            link(dve.tensor_reduce(ntile[:], over[:], AX.X, ALU.add))
            dve.tensor_copy(ntile_b[:], ntile[:].to_broadcast([NE, P])).then_inc(tiled, 1)
            dve.wait_ge(placed, 1)
            link(dve.tensor_copy(cend[:], bank[2][0:NE, 1:2]))
            dve.tensor_scalar(passed[:], tileno_sb[:], cend[:], None, ALU.is_ge).then_inc(passed_ok, 1)
            link(dve.tensor_scalar(place[:], bank[3][:, 0:NE], float(P), float(SHARED_TILES * P + 1),
                                   ALU.mult, ALU.add))
            link(dve.tensor_tensor(key[:], pair[0][:].rearrange("p (t e) -> p t e", e=NE), over_t(place[:]), ALU.add))
            link(dve.tensor_tensor(key[:], key[:], sel[:], ALU.mult))
            for t in range(NT):
                last = dve.max(top[:, t], key[:, t])
            link(last)
            link(dve.tensor_scalar_add(slot_f[:], top[:], -1.0))
            dve.tensor_copy(slot_i[:], slot_f[:])
            dve.tensor_scalar_add(slot_r[:], slot_f[:], float(-SHARED_TILES * P)).then_inc(slots_ok, 1)
            for e in range(SHARED):
                dve.memset(tile_ef[:, e * NT:(e + 1) * NT], float(e))
                dve.memset(last_tf[:, e:e + 1], float((e + 1) * NT))
            dve.wait_ge(ended, 1)
            dve.tensor_scalar(tile_ef[:, SHARED_TILES:TILES], bank[2][0:1, 128:128 + ROUTED_TILES], float(SHARED),
                              float(XT - 1), ALU.add, ALU.min)
            link(dve.tensor_scalar_add(last_tf[:, SHARED:XT], bank[2][0:1, 64:64 + NE], float(SHARED_TILES)))
            dve.tensor_copy(tile_e[:], tile_ef[:])
            dve.tensor_copy(last_t[:], last_tf[:]).then_inc(tables_ok, 1)
            for k in range(TOPK):
                link(dve.tensor_tensor(tmp[:], key[:], over_e(top[:, :, k]), ALU.is_equal))
                link(dve.tensor_tensor(tmp[:], tmp[:], comb[:], ALU.mult))
                link(dve.tensor_reduce(w6[:, :, k], tmp[:], AX.X, ALU.add))
            for e in range(SHARED):
                last = dve.tensor_copy(idx_all[:, e * NT:(e + 1) * NT], tok_sb[:])
            last.then_inc(idx_ok, 1)

            def maxes(m, n):
                p, qt = n % 2, n // NG
                dve.wait_ge(s_ok, m + 1)
                dve.tensor_reduce(negm[:, p], pair[p][:].rearrange("p (h k) -> p h k", h=G)[:, :, 0:(qt + 1) * P],
                                  AX.X, ALU.max, negate=True).then_inc(max_ok, 1)

            def pT_copy(m, n):
                p, qt = n % 2, n // NG
                if not (isinstance(m, int) and m < 2):
                    dve.wait_ge(av_ok, m - 1)
                k = 2 * (qt + 1)
                for half in range(2):
                    dve.wait_ge(pt_ok, 2 * m + half + 1)
                    dve.tensor_copy(pT[:, p, k * half:k * (half + 1), :],
                                    bank[half][:, 0:k * P].rearrange("p (k q) -> p k q", k=k)).then_inc(pt_taken, 1)

            def normalise(c, qt):
                dve.wait_ge(av_ok, NG * (c + 1))
                dve.reciprocal(rrec[:, qt], rsum[:, qt]).then_inc(drec, 1)
                dve.wait_ge(drec, c + 1)
                dve.tensor_tensor(on[:, qt].rearrange("p (h d) -> p h d", d=D),
                                  bank[2 + qt][:, 0:E].rearrange("p (h d) -> p h d", d=D),
                                  rrec[:, qt].unsqueeze(2).to_broadcast([P, H, D]), ALU.mult).then_inc(on_ok, 1)

            def residual(c, qt):
                dve.wait_ge(wo_ok, c + 1)
                xa = x_all[:, bass.ds(c, 1), :].rearrange("p o e -> p (o e)")
                dve.tensor_tensor(xa, xa, bank[2 + qt][:, 0:E], ALU.add).then_inc(res_ok, 1)

            dve.wait_ge(resid_ok, NT)

            def d_step(b, n, first, last_b):
                u = n // UNITS
                m, n = UNITS * b + n, n % UNITS
                if not (last_b and n == UNITS - 1):
                    maxes(m + 1, (n + 1) % UNITS)
                pT_copy(m, n)
                if n % NG == 0 and not (first and n == 0):
                    normalise(SB * (b + u) + (0 if n else -1), 0 if n else 1)
                if n % NG == 3 and not (first and n == 3):
                    residual(SB * (b + u) + (0 if n == 7 else -1), 0 if n == 7 else 1)

            maxes(0, 0)
            attention(dve, d_step)
            normalise(SB * B - 1, 1)
            residual(SB * B - 1, 1)

            dve.wait_ge(stokT, 1)
            dve.tensor_copy(idx_all[:, SHARED_TILES:TILES], bank[0][:, 0:ROUTED_TILES]).then_inc(idx_ok, 1)

            def hidden(i, u):
                dve.wait_ge(silu_ok, i + 1)
                if not (isinstance(i, int) and i < 2):
                    dve.wait_ge(at_ok, i - 1)
                dve.tensor_tensor(hid[:, u % 2], sg[:, u % 2], pair[u % 2][:, F:2 * F], ALU.mult).then_inc(hid_ok, 1)

            def hT_copy(i, u):
                dve.wait_ge(at_ok, i + 1)
                if not (isinstance(i, int) and i < 2):
                    dve.wait_ge(dn_ok, i - 1)
                dve.tensor_copy(hT[:, u % 2], bank[2 + u % 2][0:FP, 0:2 * P].rearrange("p (c t) -> p c t", c=2)
                                ).then_inc(hT_ok, 1)

            experts([(2, hidden), (1, hT_copy)], dve)

            def combine(t, u, n):
                dve.wait_ge(ysh_in[u], 16 * SHARED * n)
                dve.wait_ge(yg_in[u], 16 * TOPK * n)
                if not (isinstance(t, int) and t < 2):
                    dve.wait_ge(out_done[u], 16 * (n - 1))
                a = acc[:, u]
                base = (TOPK + SHARED - 1) * t
                dve.tensor_tensor(a, x_all[:, bass.ds(t, 1), :].rearrange("p o e -> p (o e)"), ysh[:, u, 0],
                                  ALU.add).then_inc(dcomb, 1)
                dve.wait_ge(dcomb, base + 1)
                dve.tensor_tensor(a, a, ysh[:, u, 1], ALU.add).then_inc(dcomb, 1)
                for k in range(TOPK):
                    dve.wait_ge(dcomb, base + 2 + k)
                    w = w6[:, bass.ds(t, 1), k:k + 1].rearrange("p o k -> p (o k)")
                    i = dve.scalar_tensor_tensor(a, yg[:, u, k], w, a, ALU.mult, ALU.add)
                    i.then_inc(acc_ok if k == TOPK - 1 else dcomb, 1)

            for t in range(2):
                combine(t, t, 1)
            with dve.Fori(1, NT // 2) as j:
                for u in range(2):
                    combine(2 * j + u, u, j + 1)

        @block.tensor
        def _(pe):
            pe.wait_ge(c_in_act, 16 * 8)
            pe.wait_ge(consts_b, 1)

            def xn_transpose(t, u):
                pe.wait_ge(ln_ok, t + 1)
                if not (isinstance(t, int) and t < 2):
                    pe.wait_ge(xnT_ok, t - 1)
                for c in range(EC):
                    last = pe.transpose(bank[u][:, c * P:(c + 1) * P], xn[:, u, c * P:(c + 1) * P], id_f[:])
                last.then_inc(xt_ok, 1)

            def project(t, u):
                pe.wait_ge(xnT_ok, t + 1)
                if not (isinstance(t, int) and t < 2):
                    pe.wait_ge(qkv_taken, t - 1)
                    pe.wait_ge(v_ok, t - 1)
                    pe.wait_ge(logit_ok, t - 1)
                for o, w in ((pair[u][:, 0:QK], wqkv_sb[:, :, 0:QK]), (pair[u][:, 512:512 + E], wqkv_sb[:, :, QK:QK + E]),
                             (bank[2 + u][:, 0:NE], wr_sb[:])):
                    for c in range(EC):
                        last = pe.matmul(o, xnT[:, u, c], w[:, c], start=c == 0, stop=c == EC - 1)
                last.then_inc(proj_ok, 1)

            pe.wait_ge(w_in, 32)
            xn_transpose(0, 0)
            for t in range(2):
                xn_transpose(t + 1, 1 - t)
                project(t, t)
            with pe.Fori(1, NT // 2 - 1) as j:
                for u in range(2):
                    xn_transpose(2 * j + u + 1, 1 - u)
                    project(2 * j + u, u)
            xn_transpose(NT - 1, 1)
            project(NT - 2, 0)
            project(NT - 1, 1)

            pe.wait_ge(chosen, 1)
            pe.wait_ge(ones_ok, 1)
            for h in range(2):
                o = pair[0][:, 512 * h:512 * (h + 1)]
                t0, t1 = NT // 2 * h, NT // 2 * (h + 1)
                pe.matmul(o, tri_b[:], sel_b[:, t0:t1].rearrange("p t e -> p (t e)"), start=True, stop=False)
                pe.matmul(o, ones_b[:], run_b[:, t0:t1].rearrange("p t e -> p (t e)"), start=False, stop=True)
            pe.matmul(bank[2][0:NE, 0:1], run_b[:, NT], ones_b[:, 0:1], start=True, stop=True).then_inc(counted, 1)
            pe.wait_ge(tiled, 1)
            pe.matmul(bank[3][:, 0:NE], ntile_b[:], before_sb[:], start=True, stop=True)
            pe.matmul(bank[2][0:NE, 1:2], upto_sb[:], ntile[:], start=True, stop=True)
            pe.matmul(bank[2][0:1, 64:64 + NE], ntile[:], upto_sb[:], start=True, stop=True).then_inc(placed, 1)
            pe.wait_ge(passed_ok, 1)
            pe.matmul(bank[2][0:1, 128:128 + ROUTED_TILES], ones_c[:], passed[:], start=True, stop=True
                      ).then_inc(ended, 1)
            pe.wait_ge(tables_ok, 1)
            pe.wait_ge(slots_ok, 1)

            def tq(b, u, r, m):
                s, qk = r // 2, r % 2
                if r == 0:
                    pe.wait_ge(qkp_ok, SB * (b + 1))
                if m is not None:
                    pe.wait_ge(pt_taken, 2 * (m - 1) + 1 + r % 2)
                elif r >= 2:
                    pe.wait_ge(tq_taken, r - 1)
                for g in range(NG):
                    last = pe.transpose(bank[r % 2][:, g * P:(g + 1) * P],
                                        qkp[:, u, s, qk, g * G:(g + 1) * G, :].rearrange("p h d -> p (h d)"), id_f[:])
                last.then_inc(tq_ok, 1)

            def scores(m, n, b, u, first):
                p, qt, g = n % 2, n // NG, n % NG
                if n == 0:
                    pe.wait_ge(tq_taken, 4 * (b + 1))
                if not first:
                    pe.wait_ge(exp_done, m - 1)
                for h in range(G):
                    o = pair[p][:, h * S:(h + 1) * S]
                    pe.matmul(o[:, 0:(qt + 1) * P], qT[:, u, g, qt * P:(qt + 1) * P], kT[:, u, g, h, 0:(qt + 1) * P],
                              start=True, stop=False)
                    last = pe.matmul(o[:, qt * P:(qt + 1) * P], id_b[:], mask_b[:], start=False, stop=True)
                last.then_inc(s_ok, 1)

            def p_transpose(m, n, tq_round):
                p, qt = n % 2, n // NG
                pe.wait_ge(exp_done, m + 1)
                for half in range(2):
                    if not (isinstance(m, int) and m < 1):
                        pe.wait_ge(pt_taken, 2 * (m - 1) + half + 1)
                    if tq_round is not None and half == tq_round[1] % 2:
                        pe.wait_ge(tq_taken, 4 * tq_round[0] + tq_round[1] + 1)
                    i = 0
                    for h in range(2 * half, 2 * half + 2):
                        for kb in range(qt + 1):
                            last = pe.transpose(bank[half][:, i * P:(i + 1) * P],
                                                prb[:, p, h, kb * P:(kb + 1) * P], id_f[:])
                            i += 1
                    last.then_inc(pt_ok, 1)

            def values(m, n, b, first2):
                p, qt, g = n % 2, n // NG, n % NG
                pe.wait_ge(pt_taken, 2 * m + 2)
                if g == 0 and not first2:
                    pe.wait_ge(res_ok, SB * b + qt - 1)
                for h in range(G):
                    o = (g * G + h) * D
                    for kb in range(qt + 1):
                        vb = v_all[:, bass.ds(SB * b + kb, 1), o:o + D].rearrange("p o d -> p (o d)")
                        last = pe.matmul(bank[2 + qt][:, o:o + D], pT[:, p, h * (qt + 1) + kb, :], vb,
                                         start=kb == 0, stop=kb == qt)
                last.then_inc(av_ok, 1)

            def o_transpose(c, qt):
                pe.wait_ge(on_ok, c + 1)
                for k in range(EC):
                    last = pe.transpose(bank[2 + qt][:, E + k * P:E + (k + 1) * P], on[:, qt, k * P:(k + 1) * P], id_f[:])
                last.then_inc(ot_ok, 1)

            def o_project(c, qt):
                pe.wait_ge(ot_taken, c + 1)
                for k in range(EC):
                    last = pe.matmul(bank[2 + qt][:, 0:E], oT[:, qt, k], wo_sb[:, k], start=k == 0, stop=k == EC - 1)
                last.then_inc(wo_ok, 1)

            def p_step(b, n, first, last_b):
                u = n // UNITS
                m, n, bb = UNITS * b + n, n % UNITS, b + u
                if not (last_b and n == UNITS - 1):
                    nu = 1 - u if n == UNITS - 1 else u
                    scores(m + 1, (n + 1) % UNITS, bb + (1 if n == UNITS - 1 else 0), nu, first and n == 0)
                rnd = None
                if 2 <= n < 6 and not last_b:
                    rnd = (bb + 1, n - 2)
                    tq(bb + 1, 1 - u, n - 2, m)
                if not (first and n == 0):
                    values(m - 1, (n - 1) % UNITS, bb - (1 if n == 0 else 0), first)
                if n % NG == 2 and not (first and n == 2):
                    o_transpose(SB * bb + (0 if n == 6 else -1), 0 if n == 6 else 1)
                p_transpose(m, n, rnd)
                if n % NG == 3 and not (first and n == 3):
                    o_project(SB * bb + (0 if n == 7 else -1), 0 if n == 7 else 1)

            for r in range(4):
                tq(0, 0, r, None)
            scores(0, 0, 0, 0, True)
            attention(pe, p_step)
            values(UNITS * B - 1, UNITS - 1, B - 1, False)
            o_transpose(SB * B - 1, 1)
            o_project(SB * B - 1, 1)
            pe.wait_ge(res_ok, SB * B)

            pe.wait_ge(stok_in, 16)
            n = ROUTED_TILES // 2
            for c in range(2):
                last = pe.transpose(bank[0][:, c * n:(c + 1) * n], stok[:, c], id_f[0:n, 0:n])
            last.then_inc(stokT, 1)
            pe.wait_ge(idx_ok, 2)

            def x_transpose(i, u):
                pe.wait_ge(xg_in[u], 16 * (i // XB + 1) if isinstance(i, int) else (i - u) * 4 + 16)
                if not (isinstance(i, int) and i < 2):
                    pe.wait_ge(xgT_ok, i - 1)
                for c in range(EC):
                    last = pe.transpose(bank[u % 2][:, c * P:(c + 1) * P], xg[:, u, c * P:(c + 1) * P], id_f[:])
                last.then_inc(xt_done, 1)

            def up(i, u):
                e = expert_of(i)
                pe.wait_ge(xgT_ok, i + 1)
                if not (isinstance(i, int) and i < 2):
                    pe.wait_ge(hid_ok, i - 1)
                pe.wait_ge(w_ready, e + 1)
                for c in range(EC):
                    w = wgu_sb[:, bass.ds(e % WB, 1), c, :].rearrange("p o n -> p (o n)")
                    last = pe.matmul(pair[u % 2][:, 0:2 * F], xgT[:, u % 2, c], w, start=c == 0, stop=c == EC - 1)
                last.then_inc(gu_ok, 1)

            def expert_of(i):
                return pe.value_load(tile_e[0:1, bass.ds(i, 1)], min_val=0, max_val=XT - 1)

            def h_transpose(i, u):
                pe.wait_ge(hid_ok, i + 1)
                if not (isinstance(i, int) and i < 2):
                    pe.wait_ge(hT_ok, i - 1)
                for c in range(2):
                    last = pe.transpose(bank[2 + u % 2][0:FP, c * P:(c + 1) * P], hid[:, u % 2, c * FP:(c + 1) * FP],
                                        id_f[:])
                last.then_inc(at_ok, 1)

            def down(i, u):
                e = expert_of(i)
                pe.wait_ge(hT_ok, i + 1)
                if not (isinstance(i, int) and i < 2):
                    pe.wait_ge(y_ok, i - 1)
                for c in range(2):
                    w = wdn_sb[:, bass.ds(e % WB, 1), c, :].rearrange("p o n -> p (o n)")
                    last = pe.matmul(pair[u % 2][:, 512:512 + E], hT[:, u % 2, c], w, start=c == 0, stop=c == 1)
                last.then_inc(dn_ok, 1)

            experts([(3, x_transpose), (2, up), (1, h_transpose), (0, down)], pe)


def _tables():
    import numpy as np
    pos = np.arange(S, dtype=np.float32)[:, None]
    exps = -np.arange(0, D, 2, dtype=np.float32) / np.float32(D)
    theta = np.repeat(np.power(np.float32(10000.0), exps), 2)
    angle = pos * theta[None, :]
    cos, sin = np.cos(angle), np.sin(angle)
    sin[:, 0::2] *= -1.0
    rope = np.stack([cos, sin], 1)[:, :, None, :] * np.array([D ** -0.5, 1.0], np.float32)[None, None, :, None]
    r, c = np.arange(P)[:, None], np.arange(P)[None, :]
    e = np.arange(NE)
    f = np.float32
    return {
        "rope": rope.reshape(SB, P, 2, 2, D).transpose(1, 0, 2, 3, 4).astype(f).copy(),
        "tri": (r < c).astype(f), "ident": (r == c).astype(f), "mask": np.where(c > r, MASKED, 0.0).astype(f),
        "before": (e[:, None] < e[None, :]).astype(f), "upto": (e[:, None] <= e[None, :]).astype(f),
        "tileno": np.tile(np.arange(ROUTED_TILES, dtype=f), (NE, 1)),
        "thr": np.tile(P * np.arange(NT, dtype=f), (NE, 1)),
        "tok": (np.arange(NT)[None, :] * P + np.arange(P)[:, None]).astype(f),
    }


def kernel(**inputs):
    import numpy as np
    import concourse.bacc as bacc
    from concourse.bass_utils import run_bass_kernel_spmd

    a = {k: np.asarray(v) for k, v in inputs.items()}
    sgu = a["L0_ffn_ws_gate_up"].reshape(2, SHARED, F, E).transpose(1, 0, 2, 3).reshape(SHARED, 2 * F, E)
    sdn = a["L0_ffn_ws_down"].reshape(E, SHARED, F).transpose(1, 0, 2)
    gu = np.concatenate([sgu, a["L0_ffn_w_gate_up"]], 0)
    dn = np.concatenate([sdn, a["L0_ffn_w_down"]], 0)
    arrays = {
        "x": a["L0_attn_x"].reshape(T, E),
        "wqkv": np.concatenate([a["L0_attn_Wq"], a["L0_attn_Wk"], a["L0_attn_Wv"]], 1),
        "bqk": np.concatenate([a["L0_attn_bq"], a["L0_attn_bk"]])[None, :],
        "bv": a["L0_attn_bv"][None, :], "bo": a["L0_attn_bo"][None, :], "wo": a["L0_attn_Wo"],
        "wr": a["L0_ffn_gate_w"].T,
        "wgu": gu.transpose(0, 2, 1).reshape(XT, EC, P, 2 * F).transpose(0, 2, 1, 3).reshape(XT, P, EC * 2 * F),
        "wdn": dn.transpose(0, 2, 1).reshape(XT, 2, FP, E).transpose(0, 2, 1, 3).reshape(XT, FP, 2 * E),
    }
    arrays.update(_tables())
    arrays = {k: np.ascontiguousarray(v) for k, v in arrays.items()}
    nc = bacc.Bacc("TRN2", target_bir_lowering=False, num_devices=1)
    args = {k: nc.dram_tensor(k, v.shape, mybir.dt.from_np(v.dtype), kind="ExternalInput").ap()
            for k, v in arrays.items()}
    out = nc.dram_tensor("out", (T, E), F32, kind="ExternalOutput").ap()
    build(nc, *[args[k] for k in ("x", "wqkv", "bqk", "bv", "bo", "wo", "wr", "wgu", "wdn", "rope", "tri", "ident",
                                  "mask", "before", "upto", "tileno", "thr", "tok")], out)
    r = run_bass_kernel_spmd(nc, [arrays], core_ids=[0])
    return r.results[0]["out"].reshape(B, S, E)
```

```python
import concourse.bass as bass
from concourse import mybir
from contextlib import ExitStack

F32 = mybir.dt.float32
BF16 = mybir.dt.bfloat16
F16 = mybir.dt.float16
I32 = mybir.dt.int32
ALU = mybir.AluOpType
ACT = mybir.ActivationFunctionType
AX = mybir.AxisListType

P = 128
B, S, E, H, D = 8, 256, 256, 16, 16
T = B * S
NT = T // P
SB = S // P
EC = E // P
NE, TOPK, F = 64, 6, 176
SHARED = 2
FP = F // 2
XT = NE + SHARED
ROUTED_TILES = (T * TOPK + NE * (P - 1)) // P + 1
SHARED_TILES = SHARED * NT
TILES = SHARED_TILES + ROUTED_TILES
HP = 32
G = 4
NG = H // G
UNITS = SB * NG
QK = 2 * H * D
LN_EPS = 1e-5
TOP_EPS = 1e-20
MASKED = -1e30
CONSTS = 9
PAIRS = 3
XNB = 4
SHIFT = P.bit_length() - 1
XB = 4
WB = 4


def build(nc, x, wqkv, bqk, bv, bo, wo, wr, wgu, wdn, rope, tri, ident, mask, before, upto, tileno, thr, tok, iota,
          out):
    assert ROUTED_TILES == 160 and TILES % XB == 0 and NT % 2 == 0
    xn_rows = nc.dram_tensor("xn_rows", (T, E), F32, kind="Internal").ap()
    y_rows = nc.dram_tensor("y_rows", (ROUTED_TILES * P, E), F32, kind="Internal").ap()

    ctx = ExitStack()
    with ctx:
        def sb(name, shape, dt=F32):
            return ctx.enter_context(nc.sbuf_tensor(name, shape, dt))

        def sem(name):
            return ctx.enter_context(nc.semaphore(name))

        wqkv_sb = sb("wqkv_sb", [P, EC, 3 * E])
        wr_sb = sb("wr_sb", [P, EC, NE])
        wo_sb = sb("wo_sb", [P, EC, E])
        bqk_sb = sb("bqk_sb", [P, QK])
        bv_sb = sb("bv_sb", [P, E])
        bo_sb = sb("bo_sb", [P, E])
        rope_sb = sb("rope_sb", [P, SB, 2, 2, D])
        tri_f = sb("tri_f", [P, P])
        tri_b = sb("tri_b", [P, P], BF16)
        ones_b = sb("ones_b", [P, P], BF16)
        id_f = sb("id_f", [P, P])
        id_b = sb("id_b", [P, P], BF16)
        mask_f = sb("mask_f", [P, P])
        mask_b = sb("mask_b", [P, P], BF16)
        before_sb = sb("before_sb", [NE, NE])
        upto_sb = sb("upto_sb", [NE, NE])
        tileno_sb = sb("tileno_sb", [NE, ROUTED_TILES])
        thr_sb = sb("thr_sb", [NE, NT])
        tok_sb = sb("tok_sb", [P, NT])
        kT = sb("kT", [P, 2, NG, G, S])
        spare = kT[:, 1].rearrange("p g h s -> p (g h s)")
        xnT = spare.rearrange("p (t c q) -> p t c q", t=NT, c=EC)
        x_all = sb("x_all", [P, NT, E])
        stats = sb("stats", [P, NT, 6])
        mv = sb("mv", [P, NT, 2])
        var = sb("var", [P, NT])
        rstd = sb("rstd", [P, NT])
        newton = sb("newton", [P, NT])
        xn = sb("xn", [P, XNB, E])
        rot = sb("rot", [P, QK])
        qk_all = sb("qk_all", [P, NT, QK])
        v_all = sb("v_all", [P, NT, E])
        prob, sel, comb, key = (kT[:, 0].rearrange("p g h s -> p (g h s)")[:, i * NT * NE:(i + 1) * NT * NE]
                                .rearrange("p (t e) -> p t e", e=NE) for i in range(4))
        tmp = sb("tmp", [P, NT, NE])
        sel_b = sb("sel_b", [P, NT, NE], BF16)
        run_b = sb("run_b", [P, NT + 1, NE], BF16)
        col = sb("col", [P, NT])
        top = sb("top", [P, NT, 8])
        wsum = sb("wsum", [P, NT])
        place = sb("place", [P, NE])
        slot_f = sb("slot_f", [P, NT, 8])
        slot_i = sb("slot_i", [P, NT, 8], I32)
        part_i = sb("part_i", [P, NT, 8], I32)
        slot_tile = sb("slot_tile", [P, NT, 8])
        slot_row = sb("slot_row", [P, NT, 8])
        iota_f = sb("iota_f", [P, ROUTED_TILES])
        iota_b = sb("iota_b", [P, ROUTED_TILES], F16)
        is_row = sb("is_row", [P, 2, TOPK, P], F16)
        is_tile = sb("is_tile", [P, 2, TOPK, ROUTED_TILES], F16)
        w6 = sb("w6", [P, NT, 8])
        cnt = sb("cnt", [NE, 1])
        over = sb("over", [NE, NT])
        ntile = sb("ntile", [NE, 1])
        ntile_b = sb("ntile_b", [NE, P])
        cend = sb("cend", [NE, 1])
        passed = sb("passed", [NE, ROUTED_TILES])
        ones_c = sb("ones_c", [NE, 1])
        tile_e = sb("tile_e", [1, TILES], I32)
        tile_ef = sb("tile_ef", [1, TILES])
        last_t = sb("last_t", [1, XT], I32)
        last_tf = sb("last_tf", [1, XT])
        idx_all = sb("idx_all", [P, TILES], I32)
        qkp = sb("qkp", [P, 2, SB, 2, H, HP])
        qT = sb("qT", [P, 2, NG, S])
        negm = sb("negm", [P, 2, G])
        prb = sb("prb", [P, 2, G, S])
        rsum = sb("rsum", [P, 2, H])
        rrec = sb("rrec", [P, 2, H])
        pT = sb("pT", [P, 2, G * SB, P])
        on = sb("on", [P, 2, E])
        oT = sb("oT", [P, 2, EC, P])
        wgu_sb = sb("wgu_sb", [P, WB, EC, 2 * F])
        wdn_sb = sb("wdn_sb", [FP, WB, 2, E])
        idx = sb("idx", [P, XB], I32)
        xg = prb[:, 0]
        y = prb[:, 1]
        xgT, hT = pT[:, :, 0:EC], pT[0:FP, :, EC:EC + 2]
        pT_flat = pT[:].rearrange("p u k q -> p u (k q)")
        sg, hid = pT_flat[:, :, 4 * P:4 * P + F], pT_flat[:, :, 6 * P:6 * P + F]
        cidx = sb("cidx", [P, 2, TOPK], I32)
        yg = [w[:, 0:TOPK * E].rearrange("p (k e) -> p k e", k=TOPK)
              for w in (wqkv_sb[:].rearrange("p c n -> p (c n)"), wgu_sb[:].rearrange("p s c n -> p (s c n)"))]

        bank = [ctx.enter_context(nc.psum_tensor(f"bank{i}", [P, 512], F32)) for i in range(4)]
        pair = [ctx.enter_context(nc.psum_tensor(f"pair{i}", [P, 1024], F32)) for i in range(2)]

        x_in = [sem(f"x_in{i}") for i in range(4)]
        w_in = sem("w_in"); c_in = sem("c_in"); c_in_act = sem("c_in_act")
        consts_b = sem("consts_b"); ones_ok = sem("ones_ok"); pad_ok = sem("pad_ok")
        var_ok = sem("var_ok"); root_ok = sem("root_ok"); ln_ok = sem("ln_ok")
        xn_out = [sem(f"xn_out{i}") for i in range(XNB)]
        xt_ok = sem("xt_ok"); xnT_ok = sem("xnT_ok"); router_ok = sem("router_ok"); logit_ok = sem("logit_ok")
        proj_ok = sem("proj_ok"); qkv_ok = sem("qkv_ok"); resid_ok = sem("resid_ok")
        dchain = sem("dchain")
        exp_in = sem("exp_in"); exp_ok = sem("exp_ok"); chosen = sem("chosen"); counted = sem("counted")
        tiled = sem("tiled"); placed = sem("placed"); passed_ok = sem("passed_ok"); ended = sem("ended")
        tables_ok = sem("tables_ok"); onehot_ok = sem("onehot_ok"); listed = sem("listed"); idx_ok = sem("idx_ok"); dpair = sem("dpair")
        w_loaded = [sem(f"w_loaded{i}") for i in range(WB)]
        w_ready = sem("w_ready"); idx_col = sem("idx_col"); po_turn = sem("po_turn"); roped = sem("roped")
        xg_in = [sem(f"xg_in{i}") for i in range(XB)]
        xt_done = sem("xt_done"); xgT_ok = sem("xgT_ok"); gu_ok = sem("gu_ok"); silu_ok = sem("silu_ok")
        hid_ok = sem("hid_ok"); at_ok = sem("at_ok"); hT_ok = sem("hT_ok"); dn_ok = sem("dn_ok")
        y_added = sem("y_added"); y_ok = sem("y_ok"); y_out = [sem(f"y_out{i}") for i in range(XB)]
        kT_clear = sem("kT_clear"); qkp_ok = sem("qkp_ok"); tq_ok = sem("tq_ok"); tq_taken = sem("tq_taken")
        s_ok = sem("s_ok"); max_ok = sem("max_ok"); exp_done = sem("exp_done"); pt_ok = sem("pt_ok")
        pt_taken = sem("pt_taken"); av_ok = sem("av_ok"); drec = sem("drec"); on_ok = sem("on_ok")
        ot_ok = sem("ot_ok"); ot_taken = sem("ot_taken"); wo_ok = sem("wo_ok"); res_ok = sem("res_ok")
        cidx_ok = sem("cidx_ok"); yg_in = [sem("yg_in0"), sem("yg_in1")]; dcomb = sem("dcomb")
        out_done = sem("out_done")

        def bc_tab(s, cs, part):
            t = rope_sb[:, s, cs, :, part::2] if part is not None else rope_sb[:, s, cs, :, :]
            n = t.shape[-1]
            return t.unsqueeze(2).to_broadcast([P, 2, H, n])

        def attention(eng, step):
            for n in range(2 * UNITS):
                step(0, n, n < UNITS, False)
            with eng.Fori(2, B - 2, 2) as b:
                for n in range(2 * UNITS):
                    step(b, n, False, False)
            for n in range(2 * UNITS):
                step(B - 2, n, False, n >= UNITS)

        def experts(eng, stages, beside=None):
            def turn(i, u, shared):
                for lead, do in stages:
                    if not isinstance(i, int) or 0 <= i + lead < TILES:
                        do(i + lead, (u + lead) % XB, shared)

            def turns(first, last):
                for i in range(first, last):
                    turn(i, i % XB, i < SHARED_TILES)

            turns(-max(lead for lead, _ in stages), XB)
            with eng.Fori(1, SHARED_TILES // XB) as j:
                for u in range(XB):
                    turn(XB * j + u, u, True)
                if beside:
                    beside(j)
            turns(SHARED_TILES, SHARED_TILES + XB)
            with eng.Fori(SHARED_TILES // XB + 1, TILES // XB - 1) as j:
                for u in range(XB):
                    turn(XB * j + u, u, False)
            turns(TILES - XB, TILES)

        def by_pairs(eng, step):
            for i in range(2):
                step(i, i, i == 0, False)
            with eng.Fori(1, NT // 2 - 1) as j:
                for u in range(2):
                    step(2 * j + u, u, False, False)
            for i in range(NT - 2, NT):
                step(i, i % 2, False, i == NT - 1)

        block = ctx.enter_context(nc.Block())

        @block.sync
        def _(sp):
            xv = x.rearrange("(t p) e -> p t e", p=P)
            q4 = NT // 4
            sp.dma_start(x_all[:, 0:q4], xv[:, 0:q4]).then_inc(x_in[0], 16)
            sp.dma_start(wqkv_sb[:], wqkv.rearrange("(c p) n -> p c n", p=P)).then_inc(w_in, 16)
            sp.dma_start(wr_sb[:], wr.rearrange("(c p) n -> p c n", p=P)).then_inc(w_in, 16)
            for i in range(1, 4):
                sp.dma_start(x_all[:, q4 * i:q4 * (i + 1)], xv[:, q4 * i:q4 * (i + 1)]).then_inc(x_in[i], 16)
            sp.dma_start(wo_sb[:], wo.rearrange("(c p) n -> p c n", p=P)).then_inc(c_in, 16)
            for dst, src in ((before_sb, before), (upto_sb, upto), (tileno_sb, tileno), (thr_sb, thr)):
                sp.dma_start(dst[:], src).then_inc(c_in, 16)
            with sp.Fori(0, NT // XNB) as j:
                for u in range(XNB):
                    sp.wait_ge(ln_ok, XNB * j + u + 1)
                    sp.dma_start(xn_rows[bass.ds((XNB * j + u) * P, P), :], xn[:, u]).then_inc(xn_out[u], 16)

            def load(e, s):
                sp.dma_start(wgu_sb[:, s], wgu[bass.ds(e, 1), :, :].rearrange("o p n -> p (o n)")
                             if not isinstance(e, int) else wgu[e]).then_inc(w_loaded[s], 16)
                sp.dma_start(wdn_sb[:, s], wdn[bass.ds(e, 1), :, :].rearrange("o p n -> p (o n)")
                             if not isinstance(e, int) else wdn[e]).then_inc(w_loaded[s], 16)

            for e in range(WB):
                load(e, e)
            for e in range(WB - 1):
                sp.wait_ge(w_loaded[e], 32)
                sp.sem_inc(w_ready, 1)
            sp.wait_ge(tables_ok, 1)
            rounds = (XT - WB) // WB
            with sp.Fori(1, rounds + 1) as j:
                for s in range(WB):
                    sp.wait_ge(w_loaded[(s - 1) % WB], 32 * (j + (1 if s else 0)))
                    sp.sem_inc(w_ready, 1)
                    end = sp.value_load(last_t[0:1, bass.ds(WB * (j - 1) + s, 1)], min_val=1, max_val=TILES)
                    sp.wait_ge(dn_ok, end)
                    load(WB * j + s, s)
            for e in range(WB * (rounds + 1), XT + 1):
                sp.wait_ge(w_loaded[(e - 1) % WB], 32 * ((e - 1) // WB + 1))
                sp.sem_inc(w_ready, 1)
                if e < XT:
                    end = sp.value_load(last_t[0:1, e - WB:e - WB + 1], min_val=1, max_val=TILES)
                    sp.wait_ge(dn_ok, end)
                    load(e, e % WB)
            with sp.Fori(0, NT) as c:
                sp.wait_ge(res_ok, c + 1)
                sp.dma_start(out[bass.ds(c * P, P), :], x_all[:, bass.ds(c, 1), :].rearrange("p o e -> p (o e)")
                             ).then_inc(out_done, 16)
            sp.wait_ge(out_done, 16 * NT)
            for u in range(XNB):
                sp.wait_ge(xn_out[u], 16 * (NT // XNB))
            for u in range(XB):
                sp.wait_ge(y_out[u], 16 * (ROUTED_TILES // XB))

        @block.gpsimd
        def _(po):
            po.memset(ones_b[:], 1.0)
            po.memset(ones_c[:], 1.0).then_inc(ones_ok, 1)
            po.memset(qkp[:], 0.0).then_inc(pad_ok, 1)
            po.wait_ge(c_in_act, 16 * CONSTS)
            with po.Fori(0, NT) as t:
                po.wait_ge(ln_ok, t + 1)
                po.tensor_tensor(x_all[:, bass.ds(t, 1), :], x_all[:, bass.ds(t, 1), :],
                                 bo_sb[:].unsqueeze(1), ALU.add).then_inc(resid_ok, 1)

            def gather(i, u):
                po.tensor_copy(idx[:, u:u + 1], idx_all[:, bass.ds(i, 1)]).then_inc(idx_col, 1)
                po.wait_ge(idx_col, i + 1)
                po.sem_inc(po_turn, 1)
                po.indirect_dma_start(xg[:, u, :], None, xn_rows[:, :],
                                      bass.IndirectOffsetOnAxis(idx[:, u:u + 1], 0)).then_inc(xg_in[u], 16)

            ROPES = 6

            def rope(t, s, k):
                if not (isinstance(t, int) and t == 0 and k == 0):
                    po.wait_ge(roped, ROPES * t + k)
                    po.sem_inc(po_turn, 1)
                qk = qk_all[:, bass.ds(t, 1), :].rearrange("p o n -> p (o n)")
                v = v_all[:, bass.ds(t, 1), :].rearrange("p o n -> p (o n)")
                q4 = qk.rearrange("p (a h d) -> p a h d", a=2, h=H)
                r4 = rot[:].rearrange("p (a h d) -> p a h d", a=2, h=H)
                if k == 0:
                    i = po.tensor_tensor(qk, qk, bqk_sb[:], ALU.add)
                elif k == 1:
                    i = po.tensor_tensor(r4[:, :, :, 0::2], q4[:, :, :, 1::2], bc_tab(s, 1, 0), ALU.mult)
                elif k == 2:
                    i = po.tensor_tensor(r4[:, :, :, 1::2], q4[:, :, :, 0::2], bc_tab(s, 1, 1), ALU.mult)
                elif k == 3:
                    i = po.tensor_tensor(q4, q4, bc_tab(s, 0, None), ALU.mult)
                elif k == 4:
                    i = po.tensor_tensor(qk, qk, rot[:], ALU.add)
                else:
                    i = po.tensor_tensor(v, v, bv_sb[:], ALU.add)
                i.then_inc(roped, 1)

            per_block = TILES // NT
            assert per_block == 2 * ROPES

            def two_blocks(jj):
                for q in range(2 * per_block):
                    u = q % XB
                    if not (isinstance(jj, int) and jj == 0 and q < XB):
                        po.wait_ge(xt_done, 2 * per_block * jj + q - XB + 1)
                    gather(2 * per_block * jj + q, u)
                    if q % 2:
                        b, k = q // per_block, q % per_block // 2
                        rope(2 * jj + b, b, k)

            po.wait_ge(qkv_ok, NT)
            po.memset(kT[:, 1], 0.0).then_inc(kT_clear, 1)
            po.wait_ge(idx_ok, 1)
            for u in range(XNB):
                po.wait_ge(xn_out[u], 16 * (NT // XNB))
            two_blocks(0)
            two_blocks(1)
            po.wait_ge(dpair, PAIRS * (SHARED_TILES // XB - 1))
            po.memset(kT[:, 0], 0.0).then_inc(kT_clear, 1)
            with po.Fori(2, NT // 2) as jj:
                two_blocks(jj)

            def pads(b, u):
                for s in range(SB):
                    po.tensor_copy(qkp[:, u, s, :, :, 0:D].rearrange("p a h d -> p (a h) d"),
                                   qk_all[:, bass.ds(SB * b + s, 1), :].rearrange("p o (h d) -> p (o h) d", d=D)
                                   ).then_inc(qkp_ok, 1)

            def rows(t, u):
                po.tensor_copy(cidx[:, u, :], slot_i[:, bass.ds(t, 1), 0:TOPK].rearrange("p o k -> p (o k)")
                               ).then_inc(cidx_ok, 1)
                po.wait_ge(cidx_ok, t + 1)
                po.sem_inc(po_turn, 1)
                for k in range(TOPK):
                    po.indirect_dma_start(yg[u][:, k, :], None, y_rows[:, :],
                                          bass.IndirectOffsetOnAxis(cidx[:, u, k:k + 1], 0)).then_inc(yg_in[u], 16)

            po.wait_ge(roped, ROPES * NT)
            po.wait_ge(pad_ok, 1)
            for b in range(2):
                pads(b, b)
            for s in range(XB):
                po.wait_ge(y_out[s], 16 * (ROUTED_TILES // XB))
            for u in range(2):
                rows(u, u)
            with po.Fori(1, B // 2) as j:
                b = 2 * j
                for u in range(2):
                    po.wait_ge(tq_ok, 4 * (b + u) - 4)
                    pads(b + u, u)
                    for s in range(SB):
                        po.wait_ge(dcomb, TOPK * (SB * (b + u - 2) + s + 1))
                        rows(SB * (b + u - 1) + s, s)
            for s in range(SB):
                po.wait_ge(dcomb, TOPK * (SB * (B - 2) + s + 1))
                rows(SB * (B - 1) + s, s)

        @block.scalar
        def _(act):
            act.dma_start(id_f[:], ident).then_inc(c_in_act, 16)
            act.dma_start(bqk_sb[:], bqk.to_broadcast([P, QK])).then_inc(c_in_act, 16)
            act.dma_start(bv_sb[:], bv.to_broadcast([P, E])).then_inc(c_in_act, 16)
            act.dma_start(bo_sb[:], bo.to_broadcast([P, E])).then_inc(c_in_act, 16)
            act.dma_start(rope_sb[:], rope).then_inc(c_in_act, 16)
            act.dma_start(tri_f[:], tri).then_inc(c_in_act, 16)
            act.dma_start(mask_f[:], mask).then_inc(c_in_act, 16)
            act.dma_start(tok_sb[:], tok).then_inc(c_in_act, 16)
            act.dma_start(iota_f[:], iota).then_inc(c_in_act, 16)
            act.wait_ge(var_ok, 1)
            act.activation(rstd[:], var[:], ACT.Sqrt).then_inc(root_ok, 1)
            def xnT_copy(t):
                act.wait_ge(xt_ok, t + 1)
                act.activation(xnT[:, t], bank[t % 2][:, 0:E].rearrange("p (c t) -> p c t", c=EC),
                               ACT.Copy).then_inc(xnT_ok, 1)

            def logits(t):
                act.wait_ge(router_ok, t + 1)
                act.activation(prob[:, t], bank[2 + t % 2][:, 0:NE], ACT.Copy).then_inc(logit_ok, 1)

            for t in range(NT + 1):
                if t < NT:
                    xnT_copy(t)
                if t:
                    logits(t - 1)
            act.wait_ge(exp_in, 1)
            act.activation(prob[:], prob[:], ACT.Exp).then_inc(exp_ok, 1)
            for t in range(NT):
                act.wait_ge(proj_ok, t + 1)
                act.activation(qk_all[:, t], pair[t % 2][:, 0:QK], ACT.Copy)
                act.activation(v_all[:, t], pair[t % 2][:, QK:QK + E], ACT.Copy).then_inc(qkv_ok, 1)

            def xgT_copy(i, u, shared):
                act.wait_ge(xt_done, i + 1)
                if not (isinstance(i, int) and i < 2):
                    act.wait_ge(gu_ok, i - 1)
                act.activation(xgT[:, u % 2], bank[u % 2][:, 0:E].rearrange("p (c t) -> p c t", c=EC),
                               ACT.Copy).then_inc(xgT_ok, 1)

            def silu(i, u, shared):
                act.wait_ge(gu_ok, i + 1)
                if not (isinstance(i, int) and i < 2):
                    act.wait_ge(hid_ok, i - 1)
                act.activation(sg[:, u % 2], pair[u % 2][:, 0:F], ACT.Silu).then_inc(silu_ok, 1)

            def y_copy(i, u, shared):
                if shared:
                    return
                r = i - SHARED_TILES
                act.wait_ge(dn_ok, i + 1)
                if not (isinstance(i, int) and r < XB):
                    act.wait_ge(y_out[u], 16 // XB * (r - u))
                act.activation(y[:, u], pair[u % 2][:, 512:512 + E], ACT.Copy).then_inc(y_ok, 1)
                act.wait_ge(y_ok, r + 1)
                act.dma_start(y_rows[bass.ds(r * P, P), :], y[:, u]).then_inc(y_out[u], 16)

            experts(act, [(3, xgT_copy), (2, silu), (0, y_copy)])

            def tq_copy(b, u, r):
                s, qk = r // 2, r % 2
                act.wait_ge(tq_ok, 4 * b + r + 1)
                src = bank[r % 2][:].rearrange("p (g t) -> p g t", g=NG)
                if not qk:
                    last = act.activation(qT[:, u, :, s * P:(s + 1) * P], src, ACT.Copy)
                for h in range(G if qk else 0):
                    own = slice(h * HP, (h + 1) * HP)
                    last = act.activation(kT[own, u, :, h, s * P:(s + 1) * P], src[own], ACT.Copy)
                last.then_inc(tq_taken, 1)

            def exps(m, n, first):
                p, qt, g = n % 2, n // NG, n % NG
                act.wait_ge(max_ok, m + 1)
                if not first:
                    act.wait_ge(pt_ok, 2 * (m - 1))
                for h in range(G):
                    last = act.activation(prb[:, p, h, 0:(qt + 1) * P],
                                          pair[p][:, h * S:h * S + (qt + 1) * P], ACT.Exp,
                                          bias=negm[:, p, h:h + 1], accum_out=rsum[:, qt, g * G + h:g * G + h + 1])
                last.then_inc(exp_done, 1)

            def oT_copy(c, qt):
                act.wait_ge(ot_ok, c + 1)
                act.activation(oT[:, qt], bank[2 + qt][:, E:2 * E].rearrange("p (c t) -> p c t", c=EC),
                               ACT.Copy).then_inc(ot_taken, 1)

            def a_step(b, n, first, last_b):
                u = n // UNITS
                m, n = UNITS * b + n, n % UNITS
                if 2 <= n < 6 and not last_b:
                    tq_copy(b + u + 1, 1 - u, n - 2)
                if not (last_b and n == UNITS - 1):
                    exps(m + 1, (n + 1) % UNITS, first and n == 0)
                if n % NG == 2 and not (first and n == 2):
                    oT_copy(SB * (b + u) + (0 if n == 6 else -1), 0 if n == 6 else 1)

            act.wait_ge(kT_clear, 2)
            for u in range(XB):
                act.wait_ge(y_out[u], 16 * (ROUTED_TILES // XB))
            for r in range(4):
                tq_copy(0, 0, r)
            exps(0, 0, True)
            attention(act, a_step)
            oT_copy(SB * B - 1, 1)

        @block.vector
        def _(dve):
            links = [0]

            def link(i):
                links[0] += 1
                i.then_inc(dchain, 1)
                dve.wait_ge(dchain, links[0])

            dve.wait_ge(c_in_act, 16 * CONSTS)
            dve.tensor_copy(id_b[:], id_f[:])
            dve.tensor_copy(tri_b[:], tri_f[:])
            dve.tensor_copy(mask_b[:], mask_f[:])
            dve.tensor_copy(iota_b[:], iota_f[:])
            dve.memset(run_b[:, 0], 0.0).then_inc(consts_b, 1)
            def layernorm(t):
                u = t % XNB
                if t >= XNB:
                    dve.wait_ge(xt_ok, t - XNB + 1)
                    dve.wait_ge(xn_out[u], 16 * (t // XNB))
                dve.tensor_scalar(xn[:, u], x_all[:, t], mv[:, t, 0:1], rstd[:, t:t + 1], ALU.subtract, ALU.mult
                                  ).then_inc(ln_ok, 1)

            for t in range(NT):
                dve.wait_ge(x_in[t // (NT // 4)], 16)
                last = dve.bn_stats(stats[:, t], x_all[:, t])
            link(last)
            for t in range(NT):
                last = dve.bn_aggr(mv[:, t], stats[:, t])
            link(last)
            link(dve.tensor_scalar_add(var[:], mv[:, :, 1], LN_EPS))
            dve.sem_inc(var_ok, 1)
            dve.wait_ge(root_ok, 1)
            link(dve.reciprocal(rstd[:], rstd[:]))
            link(dve.tensor_tensor(newton[:], rstd[:], rstd[:], ALU.mult))
            link(dve.tensor_tensor(newton[:], newton[:], var[:], ALU.mult))
            link(dve.tensor_scalar(newton[:], newton[:], -0.5, 1.5, ALU.mult, ALU.add))
            link(dve.tensor_tensor(rstd[:], rstd[:], newton[:], ALU.mult))
            for t in range(NT):
                layernorm(t)

            def over_e(a):
                return a.unsqueeze(2).to_broadcast([P, NT, NE])

            def over_t(a):
                return a.unsqueeze(1).to_broadcast([P, NT, NE])

            dve.wait_ge(logit_ok, NT)
            link(dve.tensor_reduce(col[:], prob[:], AX.X, ALU.max, negate=True))
            dve.tensor_tensor(prob[:], prob[:], over_e(col[:]), ALU.add).then_inc(exp_in, 1)
            dve.wait_ge(exp_ok, 1)
            link(dve.tensor_reduce(col[:], prob[:], AX.X, ALU.add))
            link(dve.reciprocal(col[:], col[:]))
            link(dve.tensor_tensor(prob[:], prob[:], over_e(col[:]), ALU.mult))
            for t in range(NT):
                last = dve.max(top[:, t], prob[:, t])
            link(last)
            link(dve.tensor_reduce(wsum[:], top[:, :, 0:TOPK], AX.X, ALU.add))
            link(dve.tensor_scalar_add(wsum[:], wsum[:], TOP_EPS))
            link(dve.reciprocal(wsum[:], wsum[:]))
            sixth = over_e(top[:, :, TOPK - 1])
            link(dve.tensor_tensor(sel[:], prob[:], sixth, ALU.is_gt))
            link(dve.tensor_reduce(col[:], sel[:], AX.X, ALU.add))
            link(dve.tensor_scalar(col[:], col[:], -1.0, float(TOPK), ALU.mult, ALU.add))
            link(dve.tensor_tensor(tmp[:], prob[:], sixth, ALU.is_equal))
            for t in range(NT):
                last = dve.tensor_tensor_scan(key[:, t], tmp[:, t], tmp[:, t], 0.0, ALU.add, ALU.max)
            link(last)
            link(dve.tensor_tensor(key[:], key[:], over_e(col[:]), ALU.is_le))
            link(dve.tensor_tensor(key[:], key[:], tmp[:], ALU.mult))
            link(dve.tensor_tensor(sel[:], sel[:], key[:], ALU.add))
            link(dve.tensor_tensor(comb[:], prob[:], sel[:], ALU.mult))
            link(dve.tensor_tensor(comb[:], comb[:], over_e(wsum[:]), ALU.mult))
            link(dve.tensor_copy(sel_b[:], sel[:]))
            for t in range(NT):
                link(dve.tensor_tensor(run_b[:, t + 1], run_b[:, t], sel_b[:, t], ALU.add))
            dve.sem_inc(chosen, 1)
            dve.wait_ge(counted, 1)
            link(dve.tensor_copy(cnt[:], bank[2][0:NE, 0:1]))
            dve.wait_ge(c_in, 16 * 5)
            link(dve.tensor_scalar(over[:], thr_sb[:], cnt[:], None, ALU.is_lt))
            link(dve.tensor_reduce(ntile[:], over[:], AX.X, ALU.add))
            dve.tensor_copy(ntile_b[:], ntile[:].to_broadcast([NE, P])).then_inc(tiled, 1)
            dve.wait_ge(placed, 1)
            link(dve.tensor_copy(cend[:], bank[2][0:NE, 1:2]))
            dve.tensor_scalar(passed[:], tileno_sb[:], cend[:], None, ALU.is_ge).then_inc(passed_ok, 1)
            link(dve.tensor_scalar(place[:], bank[3][:, 0:NE], float(P), 1.0, ALU.mult, ALU.add))
            link(dve.tensor_tensor(key[:], pair[0][:].rearrange("p (t e) -> p t e", e=NE), over_t(place[:]), ALU.add))
            link(dve.tensor_tensor(key[:], key[:], sel[:], ALU.mult))
            for t in range(NT):
                last = dve.max(top[:, t], key[:, t])
            link(last)
            link(dve.tensor_scalar_add(slot_f[:], top[:], -1.0))
            link(dve.tensor_copy(slot_i[:], slot_f[:]))
            link(dve.tensor_scalar(part_i[:], slot_i[:], P - 1, None, ALU.bitwise_and))
            link(dve.tensor_copy(slot_row[:], part_i[:]))
            link(dve.tensor_scalar(part_i[:], slot_i[:], SHIFT, None, ALU.arith_shift_right))
            link(dve.tensor_copy(slot_tile[:], part_i[:]))
            for e in range(SHARED):
                dve.memset(tile_ef[:, e * NT:(e + 1) * NT], float(e))
                dve.memset(last_tf[:, e:e + 1], float((e + 1) * NT))
            dve.wait_ge(ended, 1)
            dve.tensor_scalar(tile_ef[:, SHARED_TILES:TILES], bank[2][0:1, 128:128 + ROUTED_TILES], float(SHARED),
                              float(XT - 1), ALU.add, ALU.min)
            link(dve.tensor_scalar_add(last_tf[:, SHARED:XT], bank[2][0:1, 64:64 + NE], float(SHARED_TILES)))
            dve.tensor_copy(tile_e[:], tile_ef[:])
            dve.tensor_copy(last_t[:], last_tf[:]).then_inc(tables_ok, 1)
            def one_hot(t, u, first, last):
                if not (isinstance(t, int) and t < 2):
                    dve.wait_ge(listed, t - 1)
                for k in range(TOPK):
                    dve.tensor_scalar(is_row[:, u, k], iota_b[:, 0:P],
                                      slot_row[:, bass.ds(t, 1), k:k + 1].rearrange("p o k -> p (o k)"),
                                      None, ALU.is_equal)
                    last_k = dve.tensor_scalar(is_tile[:, u, k], iota_b[:],
                                               slot_tile[:, bass.ds(t, 1), k:k + 1].rearrange("p o k -> p (o k)"),
                                               tok_sb[:, bass.ds(t, 1)], ALU.is_equal, ALU.mult)
                last_k.then_inc(onehot_ok, 1)

            by_pairs(dve, one_hot)
            for e in range(SHARED):
                dve.tensor_copy(idx_all[:, e * NT:(e + 1) * NT], tok_sb[:])
            dve.wait_ge(listed, NT)
            dve.tensor_copy(idx_all[:, SHARED_TILES:TILES], pair[1][:, 0:ROUTED_TILES]).then_inc(idx_ok, 1)

            def hidden(i, u, shared):
                dve.wait_ge(silu_ok, i + 1)
                if not (isinstance(i, int) and i < 2):
                    dve.wait_ge(at_ok, i - 1)
                dve.tensor_tensor(hid[:, u % 2], sg[:, u % 2], pair[u % 2][:, F:2 * F], ALU.mult).then_inc(hid_ok, 1)

            def hT_copy(i, u, shared):
                dve.wait_ge(at_ok, i + 1)
                if not (isinstance(i, int) and i < 2):
                    dve.wait_ge(dn_ok, i - 1)
                dve.tensor_copy(hT[:, u % 2], bank[2 + u % 2][0:FP, 0:2 * P].rearrange("p (c t) -> p c t", c=2)
                                ).then_inc(hT_ok, 1)

            def y_add(i, u, shared):
                if not shared:
                    return
                dve.wait_ge(dn_ok, i + 1)
                if not (isinstance(i, int) and i == 0):
                    dve.wait_ge(y_added, i)
                xa = x_all[:, bass.ds(i % NT, 1), :].rearrange("p o e -> p (o e)")
                dve.tensor_tensor(xa, xa, pair[u % 2][:, 512:512 + E], ALU.add).then_inc(y_added, 1)

            def slot_weights(j):
                k = j - 1
                dve.tensor_tensor(tmp[:], key[:], top[:, :, bass.ds(k, 1)].to_broadcast([P, NT, NE]), ALU.is_equal
                                  ).then_inc(dpair, 1)
                dve.wait_ge(dpair, PAIRS * k + 1)
                dve.tensor_tensor(tmp[:], tmp[:], comb[:], ALU.mult).then_inc(dpair, 1)
                dve.wait_ge(dpair, PAIRS * k + 2)
                dve.tensor_reduce(w6[:, :, bass.ds(k, 1)], tmp[:], AX.X, ALU.add).then_inc(dpair, 1)

            dve.wait_ge(resid_ok, NT)
            experts(dve, [(2, hidden), (1, hT_copy), (0, y_add)], slot_weights)

            def maxes(m, n):
                p, qt = n % 2, n // NG
                dve.wait_ge(s_ok, m + 1)
                dve.tensor_reduce(negm[:, p], pair[p][:].rearrange("p (h k) -> p h k", h=G)[:, :, 0:(qt + 1) * P],
                                  AX.X, ALU.max, negate=True).then_inc(max_ok, 1)

            def pT_copy(m, n):
                p, qt = n % 2, n // NG
                if not (isinstance(m, int) and m < 2):
                    dve.wait_ge(av_ok, m - 1)
                k = 2 * (qt + 1)
                for half in range(2):
                    dve.wait_ge(pt_ok, 2 * m + half + 1)
                    dve.tensor_copy(pT[:, p, k * half:k * (half + 1), :],
                                    bank[half][:, 0:k * P].rearrange("p (k q) -> p k q", k=k)).then_inc(pt_taken, 1)

            def normalise(c, qt):
                dve.wait_ge(av_ok, NG * (c + 1))
                dve.reciprocal(rrec[:, qt], rsum[:, qt]).then_inc(drec, 1)
                dve.wait_ge(drec, c + 1)
                dve.tensor_tensor(on[:, qt].rearrange("p (h d) -> p h d", d=D),
                                  bank[2 + qt][:, 0:E].rearrange("p (h d) -> p h d", d=D),
                                  rrec[:, qt].unsqueeze(2).to_broadcast([P, H, D]), ALU.mult).then_inc(on_ok, 1)

            def residual(c, qt):
                dve.wait_ge(wo_ok, c + 1)
                dve.wait_ge(dcomb, TOPK * (c + 1))
                xa = x_all[:, bass.ds(c, 1), :].rearrange("p o e -> p (o e)")
                dve.tensor_tensor(xa, xa, bank[2 + qt][:, 0:E], ALU.add).then_inc(res_ok, 1)

            def combine(t, u, slots):
                dve.wait_ge(yg_in[u], 16 * TOPK * (t // 2 + 1) if isinstance(t, int) else 8 * TOPK * (t - u) + 16 * TOPK)
                xa = x_all[:, bass.ds(t, 1), :].rearrange("p o e -> p (o e)")
                for k in slots:
                    if not (isinstance(t, int) and t == 0 and k == 0):
                        dve.wait_ge(dcomb, TOPK * t + k)
                    w = w6[:, bass.ds(t, 1), k:k + 1].rearrange("p o k -> p (o k)")
                    dve.scalar_tensor_tensor(xa, yg[u][:, k], w, xa, ALU.mult, ALU.add).then_inc(dcomb, 1)

            def d_step(b, n, first, last_b):
                u = n // UNITS
                m, n = UNITS * b + n, n % UNITS
                if not (last_b and n == UNITS - 1):
                    maxes(m + 1, (n + 1) % UNITS)
                pT_copy(m, n)
                if n % NG:
                    combine(SB * (b + u) + n // NG, n // NG, range(2 * (n % NG) - 2, 2 * (n % NG)))
                if n % NG == 0 and not (first and n == 0):
                    normalise(SB * (b + u) + (0 if n else -1), 0 if n else 1)
                if n % NG == 3 and not (first and n == 3):
                    residual(SB * (b + u) + (0 if n == 7 else -1), 0 if n == 7 else 1)

            dve.wait_ge(y_added, SHARED_TILES)
            dve.wait_ge(dpair, PAIRS * (SHARED_TILES // XB - 1))
            maxes(0, 0)
            attention(dve, d_step)
            normalise(SB * B - 1, 1)
            residual(SB * B - 1, 1)

        @block.tensor
        def _(pe):
            pe.wait_ge(c_in_act, 16 * CONSTS)
            pe.wait_ge(consts_b, 1)

            def xn_transpose(t):
                pe.wait_ge(ln_ok, t + 1)
                if t >= 2:
                    pe.wait_ge(xnT_ok, t - 1)
                for c in range(EC):
                    last = pe.transpose(bank[t % 2][:, c * P:(c + 1) * P], xn[:, t % XNB, c * P:(c + 1) * P], id_f[:])
                last.then_inc(xt_ok, 1)

            def route(t):
                pe.wait_ge(xnT_ok, t + 1)
                if t >= 2:
                    pe.wait_ge(logit_ok, t - 1)
                for c in range(EC):
                    last = pe.matmul(bank[2 + t % 2][:, 0:NE], xnT[:, t, c], wr_sb[:, c], start=c == 0, stop=c == EC - 1)
                last.then_inc(router_ok, 1)

            pe.wait_ge(w_in, 32)
            for t in range(NT + 1):
                if t < NT:
                    xn_transpose(t)
                if t:
                    route(t - 1)
            for t in range(NT):
                if t >= 2:
                    pe.wait_ge(qkv_ok, t - 1)
                for n0, n1 in ((0, QK), (QK, QK + E)):
                    for c in range(EC):
                        last = pe.matmul(pair[t % 2][:, n0:n1], xnT[:, t, c], wqkv_sb[:, c, n0:n1],
                                         start=c == 0, stop=c == EC - 1)
                last.then_inc(proj_ok, 1)

            pe.wait_ge(chosen, 1)
            pe.wait_ge(ones_ok, 1)
            pe.wait_ge(qkv_ok, NT)
            for h in range(2):
                o = pair[0][:, 512 * h:512 * (h + 1)]
                t0, t1 = NT // 2 * h, NT // 2 * (h + 1)
                pe.matmul(o, tri_b[:], sel_b[:, t0:t1].rearrange("p t e -> p (t e)"), start=True, stop=False)
                pe.matmul(o, ones_b[:], run_b[:, t0:t1].rearrange("p t e -> p (t e)"), start=False, stop=True)
            pe.matmul(bank[2][0:NE, 0:1], run_b[:, NT], ones_b[:, 0:1], start=True, stop=True).then_inc(counted, 1)
            pe.wait_ge(tiled, 1)
            pe.matmul(bank[3][:, 0:NE], ntile_b[:], before_sb[:], start=True, stop=True)
            pe.matmul(bank[2][0:NE, 1:2], upto_sb[:], ntile[:], start=True, stop=True)
            pe.matmul(bank[2][0:1, 64:64 + NE], ntile[:], upto_sb[:], start=True, stop=True).then_inc(placed, 1)
            pe.wait_ge(passed_ok, 1)
            pe.matmul(bank[2][0:1, 128:128 + ROUTED_TILES], ones_c[:], passed[:], start=True, stop=True
                      ).then_inc(ended, 1)
            pe.wait_ge(tables_ok, 1)

            def list_tokens(t, u, first, last):
                pe.wait_ge(onehot_ok, t + 1)
                for k in range(TOPK):
                    mm = pe.matmul(pair[1][:, 0:ROUTED_TILES], is_row[:, u, k], is_tile[:, u, k],
                                   start=first and k == 0, stop=last and k == TOPK - 1)
                mm.then_inc(listed, 1)

            by_pairs(pe, list_tokens)
            pe.wait_ge(idx_ok, 1)

            expert_reg = [pe.alloc_register(f"expert{u}") for u in range(XB)]

            def load_expert(i, u):
                pe.reg_load(expert_reg[u], tile_e[0:1, bass.ds(i, 1)])

            def expert_of(u):
                return pe.snap(expert_reg[u], min_val=0, max_val=XT - 1) & (P - 1)

            def x_transpose(i, u, shared):
                pe.wait_ge(xg_in[u], 16 * (i // XB + 1) if isinstance(i, int) else (i - u) * 4 + 16)
                if not (isinstance(i, int) and i < 2):
                    pe.wait_ge(xgT_ok, i - 1)
                for c in range(EC):
                    last = pe.transpose(bank[u % 2][:, c * P:(c + 1) * P], xg[:, u, c * P:(c + 1) * P], id_f[:])
                last.then_inc(xt_done, 1)

            def up(i, u, shared):
                e = expert_of(u)
                pe.wait_ge(xgT_ok, i + 1)
                if not (isinstance(i, int) and i < 2):
                    pe.wait_ge(hid_ok, i - 1)
                pe.wait_ge(w_ready, e + 1)
                for c in range(EC):
                    w = wgu_sb[:, bass.ds(e % WB, 1), c, :].rearrange("p o n -> p (o n)")
                    last = pe.matmul(pair[u % 2][:, 0:2 * F], xgT[:, u % 2, c], w, start=c == 0, stop=c == EC - 1)
                last.then_inc(gu_ok, 1)
                if not (isinstance(i, int) and i + 1 >= TILES):
                    load_expert(i + 1, (u + 1) % XB)

            def h_transpose(i, u, shared):
                pe.wait_ge(hid_ok, i + 1)
                if not (isinstance(i, int) and i < 2):
                    pe.wait_ge(hT_ok, i - 1)
                for c in range(2):
                    last = pe.transpose(bank[2 + u % 2][0:FP, c * P:(c + 1) * P], hid[:, u % 2, c * FP:(c + 1) * FP],
                                        id_f[:])
                last.then_inc(at_ok, 1)

            def down(i, u, shared):
                e = expert_of(u)
                pe.wait_ge(hT_ok, i + 1)
                if shared or isinstance(i, int) and i < SHARED_TILES + 2:
                    if not (isinstance(i, int) and i < 2):
                        pe.wait_ge(y_added, i - 1)
                else:
                    pe.wait_ge(y_ok, i - SHARED_TILES - 1)
                for c in range(2):
                    w = wdn_sb[:, bass.ds(e % WB, 1), c, :].rearrange("p o n -> p (o n)")
                    last = pe.matmul(pair[u % 2][:, 512:512 + E], hT[:, u % 2, c], w, start=c == 0, stop=c == 1)
                last.then_inc(dn_ok, 1)

            load_expert(0, 0)
            experts(pe, [(3, x_transpose), (2, up), (1, h_transpose), (0, down)])

            def tq(b, u, r, m):
                s, qk = r // 2, r % 2
                if r == 0:
                    pe.wait_ge(qkp_ok, SB * (b + 1))
                if m is not None:
                    pe.wait_ge(pt_taken, 2 * (m - 1) + 1 + r % 2)
                elif r >= 2:
                    pe.wait_ge(tq_taken, r - 1)
                for g in range(NG):
                    last = pe.transpose(bank[r % 2][:, g * P:(g + 1) * P],
                                        qkp[:, u, s, qk, g * G:(g + 1) * G, :].rearrange("p h d -> p (h d)"), id_f[:])
                last.then_inc(tq_ok, 1)

            def scores(m, n, b, u, first):
                p, qt, g = n % 2, n // NG, n % NG
                if n == 0:
                    pe.wait_ge(tq_taken, 4 * (b + 1))
                if not first:
                    pe.wait_ge(exp_done, m - 1)
                for h in range(G):
                    o = pair[p][:, h * S:(h + 1) * S]
                    pe.matmul(o[:, 0:(qt + 1) * P], qT[:, u, g, qt * P:(qt + 1) * P], kT[:, u, g, h, 0:(qt + 1) * P],
                              start=True, stop=False)
                    last = pe.matmul(o[:, qt * P:(qt + 1) * P], id_b[:], mask_b[:], start=False, stop=True)
                last.then_inc(s_ok, 1)

            def p_transpose(m, n, tq_round):
                p, qt = n % 2, n // NG
                pe.wait_ge(exp_done, m + 1)
                for half in range(2):
                    if not (isinstance(m, int) and m < 1):
                        pe.wait_ge(pt_taken, 2 * (m - 1) + half + 1)
                    if tq_round is not None and half == tq_round[1] % 2:
                        pe.wait_ge(tq_taken, 4 * tq_round[0] + tq_round[1] + 1)
                    i = 0
                    for h in range(2 * half, 2 * half + 2):
                        for kb in range(qt + 1):
                            last = pe.transpose(bank[half][:, i * P:(i + 1) * P],
                                                prb[:, p, h, kb * P:(kb + 1) * P], id_f[:])
                            i += 1
                    last.then_inc(pt_ok, 1)

            def values(m, n, b, first2):
                p, qt, g = n % 2, n // NG, n % NG
                pe.wait_ge(pt_taken, 2 * m + 2)
                if g == 0 and not first2:
                    pe.wait_ge(res_ok, SB * b + qt - 1)
                for h in range(G):
                    o = (g * G + h) * D
                    for kb in range(qt + 1):
                        vb = v_all[:, bass.ds(SB * b + kb, 1), o:o + D].rearrange("p o d -> p (o d)")
                        last = pe.matmul(bank[2 + qt][:, o:o + D], pT[:, p, h * (qt + 1) + kb, :], vb,
                                         start=kb == 0, stop=kb == qt)
                last.then_inc(av_ok, 1)

            def o_transpose(c, qt):
                pe.wait_ge(on_ok, c + 1)
                for k in range(EC):
                    last = pe.transpose(bank[2 + qt][:, E + k * P:E + (k + 1) * P], on[:, qt, k * P:(k + 1) * P], id_f[:])
                last.then_inc(ot_ok, 1)

            def o_project(c, qt):
                pe.wait_ge(ot_taken, c + 1)
                for k in range(EC):
                    last = pe.matmul(bank[2 + qt][:, 0:E], oT[:, qt, k], wo_sb[:, k], start=k == 0, stop=k == EC - 1)
                last.then_inc(wo_ok, 1)

            def p_step(b, n, first, last_b):
                u = n // UNITS
                m, n, bb = UNITS * b + n, n % UNITS, b + u
                if not (last_b and n == UNITS - 1):
                    nu = 1 - u if n == UNITS - 1 else u
                    scores(m + 1, (n + 1) % UNITS, bb + (1 if n == UNITS - 1 else 0), nu, first and n == 0)
                rnd = None
                if 2 <= n < 6 and not last_b:
                    rnd = (bb + 1, n - 2)
                    tq(bb + 1, 1 - u, n - 2, m)
                if not (first and n == 0):
                    values(m - 1, (n - 1) % UNITS, bb - (1 if n == 0 else 0), first)
                if n % NG == 2 and not (first and n == 2):
                    o_transpose(SB * bb + (0 if n == 6 else -1), 0 if n == 6 else 1)
                p_transpose(m, n, rnd)
                if n % NG == 3 and not (first and n == 3):
                    o_project(SB * bb + (0 if n == 7 else -1), 0 if n == 7 else 1)

            pe.wait_ge(y_ok, ROUTED_TILES)
            for r in range(4):
                tq(0, 0, r, None)
            scores(0, 0, 0, 0, True)
            attention(pe, p_step)
            values(UNITS * B - 1, UNITS - 1, B - 1, False)
            o_transpose(SB * B - 1, 1)
            o_project(SB * B - 1, 1)
            pe.wait_ge(res_ok, SB * B)


def _tables():
    import numpy as np
    pos = np.arange(S, dtype=np.float32)[:, None]
    exps = -np.arange(0, D, 2, dtype=np.float32) / np.float32(D)
    theta = np.repeat(np.power(np.float32(10000.0), exps), 2)
    angle = pos * theta[None, :]
    cos, sin = np.cos(angle), np.sin(angle)
    sin[:, 0::2] *= -1.0
    rope = np.stack([cos, sin], 1)[:, :, None, :] * np.array([D ** -0.5, 1.0], np.float32)[None, None, :, None]
    r, c = np.arange(P)[:, None], np.arange(P)[None, :]
    e = np.arange(NE)
    f = np.float32
    return {
        "rope": rope.reshape(SB, P, 2, 2, D).transpose(1, 0, 2, 3, 4).astype(f).copy(),
        "tri": (r < c).astype(f), "ident": (r == c).astype(f), "mask": np.where(c > r, MASKED, 0.0).astype(f),
        "before": (e[:, None] < e[None, :]).astype(f), "upto": (e[:, None] <= e[None, :]).astype(f),
        "tileno": np.tile(np.arange(ROUTED_TILES, dtype=f), (NE, 1)),
        "thr": np.tile(P * np.arange(NT, dtype=f), (NE, 1)),
        "iota": np.tile(np.arange(ROUTED_TILES, dtype=f), (P, 1)),
        "tok": (np.arange(NT)[None, :] * P + np.arange(P)[:, None]).astype(f),
    }


def kernel(**inputs):
    import numpy as np
    import concourse.bacc as bacc
    from concourse.bass_utils import run_bass_kernel_spmd

    a = {k: np.asarray(v) for k, v in inputs.items()}
    sgu = a["L0_ffn_ws_gate_up"].reshape(2, SHARED, F, E).transpose(1, 0, 2, 3).reshape(SHARED, 2 * F, E)
    sdn = a["L0_ffn_ws_down"].reshape(E, SHARED, F).transpose(1, 0, 2)
    gu = np.concatenate([sgu, a["L0_ffn_w_gate_up"]], 0)
    dn = np.concatenate([sdn, a["L0_ffn_w_down"]], 0)
    arrays = {
        "x": a["L0_attn_x"].reshape(T, E),
        "wqkv": np.concatenate([a["L0_attn_Wq"], a["L0_attn_Wk"], a["L0_attn_Wv"]], 1),
        "bqk": np.concatenate([a["L0_attn_bq"], a["L0_attn_bk"]])[None, :],
        "bv": a["L0_attn_bv"][None, :], "bo": a["L0_attn_bo"][None, :], "wo": a["L0_attn_Wo"],
        "wr": a["L0_ffn_gate_w"].T,
        "wgu": gu.transpose(0, 2, 1).reshape(XT, EC, P, 2 * F).transpose(0, 2, 1, 3).reshape(XT, P, EC * 2 * F),
        "wdn": dn.transpose(0, 2, 1).reshape(XT, 2, FP, E).transpose(0, 2, 1, 3).reshape(XT, FP, 2 * E),
    }
    arrays.update(_tables())
    arrays = {k: np.ascontiguousarray(v) for k, v in arrays.items()}
    nc = bacc.Bacc("TRN2", target_bir_lowering=False, num_devices=1)
    args = {k: nc.dram_tensor(k, v.shape, mybir.dt.from_np(v.dtype), kind="ExternalInput").ap()
            for k, v in arrays.items()}
    out = nc.dram_tensor("out", (T, E), F32, kind="ExternalOutput").ap()
    build(nc, *[args[k] for k in ("x", "wqkv", "bqk", "bv", "bo", "wo", "wr", "wgu", "wdn", "rope", "tri", "ident",
                                  "mask", "before", "upto", "tileno", "thr", "tok", "iota")], out)
    r = run_bass_kernel_spmd(nc, [arrays], core_ids=[0])
    return r.results[0]["out"].reshape(B, S, E)
```

```python
import concourse.bass as bass
from concourse import mybir
from contextlib import ExitStack

F32 = mybir.dt.float32
BF16 = mybir.dt.bfloat16
F32R = mybir.dt.float32r
F16 = mybir.dt.float16
I32 = mybir.dt.int32
ALU = mybir.AluOpType
ACT = mybir.ActivationFunctionType
AX = mybir.AxisListType

P = 128
B, S, E, H, D = 8, 256, 256, 16, 16
T = B * S
NT = T // P
SB = S // P
EC = E // P
NE, TOPK, F = 64, 6, 176
SHARED = 2
FP = F // 2
XT = NE + SHARED
ROUTED_TILES = (T * TOPK + NE * (P - 1)) // P + 1
SHARED_TILES = SHARED * NT
TILES = SHARED_TILES + ROUTED_TILES
HP = 32
G = 4
NG = H // G
UNITS = SB * NG
QK = 2 * H * D
LN_EPS = 1e-5
TOP_EPS = 1e-20
MASKED = -1e30
CONSTS = 9
LIST_TURNS = 6
EARLY = NT // 2 - LIST_TURNS
W6_TURN = SHARED_TILES // 4 + 1
SPLITS = 3
ROUNDS = ((0, 2), (0, 0), (0, 1), (1, 0), (1, 1), (1, 2))
NR = len(ROUNDS)
FIRST_BLOCK = 3
PAIRS = 3
XNB = 4
SHIFT = P.bit_length() - 1
XB = 4
WB = 4


def build(nc, x, wqkv, bqk, bv, bo, wo, wr, wgu, wdn, rope, tri, ident, mask, before, upto, tileno, thr, tok, iota,
          out):
    assert ROUTED_TILES == 160 and TILES % XB == 0 and NT % 2 == 0
    xn_rows = nc.dram_tensor("xn_rows", (T, E), F32, kind="Internal").ap()
    y_rows = nc.dram_tensor("y_rows", (ROUTED_TILES * P, E), F32, kind="Internal").ap()

    ctx = ExitStack()
    with ctx:
        def sb(name, shape, dt=F32):
            return ctx.enter_context(nc.sbuf_tensor(name, shape, dt))

        def sem(name):
            return ctx.enter_context(nc.semaphore(name))

        wqkv_sb = sb("wqkv_sb", [P, EC, 3 * E])
        wr_sb = sb("wr_sb", [P, EC, NE])
        wo_sb = sb("wo_sb", [P, EC, E])
        bqk_sb = sb("bqk_sb", [P, QK])
        bv_sb = sb("bv_sb", [P, E])
        bo_sb = sb("bo_sb", [P, E])
        rope_sb = sb("rope_sb", [P, SB, 2, 2, D])
        tri_f = sb("tri_f", [P, P])
        tri_b = sb("tri_b", [P, P], BF16)
        ones_b = sb("ones_b", [P, P], BF16)
        id_f = sb("id_f", [P, P])
        id_b = sb("id_b", [P, P], BF16)
        mask_f = sb("mask_f", [P, P])
        mask_b = sb("mask_b", [P, P], BF16)
        before_sb = sb("before_sb", [NE, NE])
        upto_sb = sb("upto_sb", [NE, NE])
        tileno_sb = sb("tileno_sb", [NE, ROUTED_TILES])
        thr_sb = sb("thr_sb", [NE, NT])
        tok_sb = sb("tok_sb", [P, NT])
        with nc.sbuf_tensor("room", [P, 2, NT * E], F32) as room:
            xnT = room[:, 1].rearrange("p (t c q) -> p t c q", t=NT, c=EC)
        kT = sb("kT", [P, 2, NG, G, S], F32R)
        with nc.sbuf_tensor("wdn_sb", [FP, WB, 2, E], F32) as wdn_sb:
            pass
        qT_hi = sb("qT_hi", [P, 2, NG, S], F32R)
        with nc.sbuf_tensor("xn", [P, XNB, E], F32) as xn, nc.sbuf_tensor("tmp", [P, NT, NE], F32) as tmp:
            pass
        qT_lo = sb("qT_lo", [P, 2, NG, S], F32R)
        assert WB * 2 * E == 2 * NG * S and XNB * E + NT * NE == 2 * NG * S and 2 * NT * E == 2 * NG * G * S
        x_all = sb("x_all", [P, NT, E])
        stats = sb("stats", [P, NT, 6])
        mv = sb("mv", [P, NT, 2])
        var = sb("var", [P, NT])
        rstd = sb("rstd", [P, NT])
        newton = sb("newton", [P, NT])
        rot = sb("rot", [P, QK])
        qk_all = sb("qk_all", [P, NT, QK])
        v_all = sb("v_all", [P, NT, E])
        prob, sel, comb, key = (room[:, 0, i * NT * NE:(i + 1) * NT * NE]
                                 .rearrange("p (t e) -> p t e", e=NE) for i in range(4))
        sel_b = sb("sel_b", [P, NT, NE], BF16)
        run_b = sb("run_b", [P, NT + 1, NE], BF16)
        col = sb("col", [P, NT])
        top = sb("top", [P, NT, 8])
        wsum = sb("wsum", [P, NT])
        place = sb("place", [P, NE])
        slot_f = sb("slot_f", [P, NT, 8])
        slot_i = sb("slot_i", [P, NT, 8], I32)
        part_i = sb("part_i", [P, NT, 8], I32)
        slot_tile = sb("slot_tile", [P, NT, 8])
        slot_row = sb("slot_row", [P, NT, 8])
        token_no = sb("token_no", [P, ROUTED_TILES])
        iota_f = sb("iota_f", [P, ROUTED_TILES])
        iota_b = sb("iota_b", [P, ROUTED_TILES], F16)
        is_row = sb("is_row", [P, 2, TOPK, P], F16)
        is_tile = sb("is_tile", [P, 2, TOPK, ROUTED_TILES], F16)
        w6 = sb("w6", [P, NT, 8])
        cnt = sb("cnt", [NE, 1])
        over = sb("over", [NE, NT])
        ntile = sb("ntile", [NE, 1])
        ntile_b = sb("ntile_b", [NE, P])
        cend = sb("cend", [NE, 1])
        passed = sb("passed", [NE, ROUTED_TILES])
        ones_c = sb("ones_c", [NE, 1])
        tile_e = sb("tile_e", [1, TILES], I32)
        tile_ef = sb("tile_ef", [1, TILES])
        last_t = sb("last_t", [1, XT], I32)
        last_tf = sb("last_tf", [1, XT])
        idx_all = sb("idx_all", [P, TILES], I32)
        qkp = sb("qkp", [P, 2, SB, 3, H, HP])
        negm = sb("negm", [P, 2, G])
        prb = sb("prb", [P, 2, G, S])
        rsum = sb("rsum", [P, 2, H])
        rrec = sb("rrec", [P, 2, H])
        pT = sb("pT", [P, 2, G * SB, P])
        on = sb("on", [P, 2, E])
        oT = sb("oT", [P, 2, EC, P])
        wgu_sb = sb("wgu_sb", [P, WB, EC, 2 * F])
        idx = sb("idx", [P, XB], I32)
        xg = prb[:, 0]
        y = prb[:, 1]
        xgT, hT = pT[:, :, 0:EC], pT[0:FP, :, EC:EC + 2]
        pT_flat = pT[:].rearrange("p u k q -> p u (k q)")
        sg, hid = pT_flat[:, :, 4 * P:4 * P + F], pT_flat[:, :, 6 * P:6 * P + F]
        cidx = sb("cidx", [P, 2, TOPK], I32)
        yg = [w[:, 0:TOPK * E].rearrange("p (k e) -> p k e", k=TOPK)
              for w in (wqkv_sb[:].rearrange("p c n -> p (c n)"), wgu_sb[:].rearrange("p s c n -> p (s c n)"))]

        bank = [ctx.enter_context(nc.psum_tensor(f"bank{i}", [P, 512], F32)) for i in range(4)]
        pair = [ctx.enter_context(nc.psum_tensor(f"pair{i}", [P, 1024], F32)) for i in range(2)]

        x_in = [sem(f"x_in{i}") for i in range(4)]
        w_in = sem("w_in"); wr_in = sem("wr_in"); c_in = sem("c_in"); c_in_act = sem("c_in_act")
        consts_b = sem("consts_b"); ones_ok = sem("ones_ok"); pad_ok = sem("pad_ok")
        var_ok = sem("var_ok"); root_ok = sem("root_ok"); ln_ok = sem("ln_ok")
        xn_out = [sem(f"xn_out{i}") for i in range(XNB)]
        xt_ok = sem("xt_ok"); xnT_ok = sem("xnT_ok"); router_ok = sem("router_ok"); logit_ok = sem("logit_ok")
        proj_ok = sem("proj_ok"); qkv_ok = sem("qkv_ok"); resid_ok = sem("resid_ok")
        dchain = sem("dchain")
        exp_in = sem("exp_in"); exp_ok = sem("exp_ok"); chosen = sem("chosen"); counted = sem("counted")
        tiled = sem("tiled"); placed = sem("placed"); passed_ok = sem("passed_ok"); ended = sem("ended")
        tables_ok = sem("tables_ok"); onehot_ok = sem("onehot_ok"); list_taken = sem("list_taken"); listed = sem("listed"); idx_ok = sem("idx_ok"); dpair = sem("dpair")
        w_loaded = [sem(f"w_loaded{i}") for i in range(WB)]
        w_ready = sem("w_ready"); idx_col = sem("idx_col"); po_turn = sem("po_turn"); roped = sem("roped")
        xg_in = [sem(f"xg_in{i}") for i in range(XB)]
        xt_done = sem("xt_done"); xgT_ok = sem("xgT_ok"); gu_ok = sem("gu_ok"); silu_ok = sem("silu_ok")
        hid_ok = sem("hid_ok"); at_ok = sem("at_ok"); hT_ok = sem("hT_ok"); dn_ok = sem("dn_ok")
        y_added = sem("y_added"); y_ok = sem("y_ok"); y_out = [sem(f"y_out{i}") for i in range(XB)]
        kT_clear = sem("kT_clear"); qkp_ok = sem("qkp_ok"); padded = sem("padded"); tq_ok = sem("tq_ok"); tq_taken = sem("tq_taken")
        s_ok = sem("s_ok"); max_ok = sem("max_ok"); exp_done = sem("exp_done"); pt_ok = sem("pt_ok")
        pt_taken = sem("pt_taken"); av_ok = sem("av_ok"); drec = sem("drec"); on_ok = sem("on_ok")
        ot_ok = sem("ot_ok"); ot_taken = sem("ot_taken"); wo_ok = sem("wo_ok"); res_ok = sem("res_ok")
        cidx_ok = sem("cidx_ok"); yg_in = [sem("yg_in0"), sem("yg_in1")]; dcomb = sem("dcomb")
        out_done = sem("out_done")

        def bc_tab(s, cs, part):
            t = rope_sb[:, s, cs, :, part::2] if part is not None else rope_sb[:, s, cs, :, :]
            n = t.shape[-1]
            return t.unsqueeze(2).to_broadcast([P, 2, H, n])

        def attention(eng, step):
            for n in range(2 * UNITS):
                step(0, n, n < UNITS, False)
            with eng.Fori(2, B - 2, 2) as b:
                for n in range(2 * UNITS):
                    step(b, n, False, False)
            for n in range(2 * UNITS):
                step(B - 2, n, False, n >= UNITS)

        def experts(eng, stages, listing=None, listed_all=None, weighing=None, ending=None):
            def turn(i, u, shared):
                for lead, do in stages:
                    if not isinstance(i, int) or 0 <= i + lead < TILES:
                        do(i + lead, (u + lead) % XB, shared)

            def turns(first, last):
                for i in range(first, last):
                    turn(i, i % XB, i < SHARED_TILES)

            turns(-max(lead for lead, _ in stages), XB)
            with eng.Fori(1, LIST_TURNS + 1) as j:
                for u in range(XB):
                    turn(XB * j + u, u, True)
                    if listing:
                        listing(j, u)
            if listed_all:
                listed_all()
            turns(XB * (LIST_TURNS + 1), SHARED_TILES + XB)
            with eng.Fori(W6_TURN, W6_TURN + TOPK + 1) as j:
                for u in range(XB):
                    turn(XB * j + u, u, False)
                if weighing:
                    weighing(j)
            with eng.Fori(W6_TURN + TOPK + 1, TILES // XB - 1) as j:
                for u in range(XB):
                    turn(XB * j + u, u, False)
            for i in range(TILES - XB, TILES):
                turn(i, i % XB, False)
                if ending:
                    ending(i % XB)

        block = ctx.enter_context(nc.Block())

        @block.sync
        def _(sp):
            xv = x.rearrange("(t p) e -> p t e", p=P)
            q4 = NT // 4
            sp.dma_start(x_all[:, 0:q4], xv[:, 0:q4]).then_inc(x_in[0], 16)
            for i in range(1, 4):
                sp.dma_start(x_all[:, q4 * i:q4 * (i + 1)], xv[:, q4 * i:q4 * (i + 1)]).then_inc(x_in[i], 16)
            sp.dma_start(wr_sb[:], wr.rearrange("(c p) n -> p c n", p=P)).then_inc(wr_in, 16)
            sp.dma_start(wqkv_sb[:], wqkv.rearrange("(c p) n -> p c n", p=P)).then_inc(w_in, 16)
            sp.dma_start(wo_sb[:], wo.rearrange("(c p) n -> p c n", p=P)).then_inc(c_in, 16)
            for dst, src in ((before_sb, before), (upto_sb, upto), (tileno_sb, tileno), (thr_sb, thr)):
                sp.dma_start(dst[:], src).then_inc(c_in, 16)
            with sp.Fori(0, NT // XNB) as j:
                for u in range(XNB):
                    sp.wait_ge(ln_ok, XNB * j + u + 1)
                    sp.dma_start(xn_rows[bass.ds((XNB * j + u) * P, P), :], xn[:, u]).then_inc(xn_out[u], 16)

            def load(e, s):
                sp.dma_start(wgu_sb[:, s], wgu[bass.ds(e, 1), :, :].rearrange("o p n -> p (o n)")
                             if not isinstance(e, int) else wgu[e]).then_inc(w_loaded[s], 16)
                sp.dma_start(wdn_sb[:, s], wdn[bass.ds(e, 1), :, :].rearrange("o p n -> p (o n)")
                             if not isinstance(e, int) else wdn[e]).then_inc(w_loaded[s], 16)

            for e in range(WB):
                load(e, e)
            for e in range(WB - 1):
                sp.wait_ge(w_loaded[e], 32)
                sp.sem_inc(w_ready, 1)
            sp.wait_ge(tables_ok, 1)
            rounds = (XT - WB) // WB
            with sp.Fori(1, rounds + 1) as j:
                for s in range(WB):
                    sp.wait_ge(w_loaded[(s - 1) % WB], 32 * (j + (1 if s else 0)))
                    sp.sem_inc(w_ready, 1)
                    end = sp.value_load(last_t[0:1, bass.ds(WB * (j - 1) + s, 1)], min_val=1, max_val=TILES)
                    sp.wait_ge(dn_ok, end)
                    load(WB * j + s, s)
            for e in range(WB * (rounds + 1), XT + 1):
                sp.wait_ge(w_loaded[(e - 1) % WB], 32 * ((e - 1) // WB + 1))
                sp.sem_inc(w_ready, 1)
                if e < XT:
                    end = sp.value_load(last_t[0:1, e - WB:e - WB + 1], min_val=1, max_val=TILES)
                    sp.wait_ge(dn_ok, end)
                    load(e, e % WB)
            with sp.Fori(0, NT) as c:
                sp.wait_ge(res_ok, c + 1)
                sp.dma_start(out[bass.ds(c * P, P), :], x_all[:, bass.ds(c, 1), :].rearrange("p o e -> p (o e)")
                             ).then_inc(out_done, 16)
            sp.wait_ge(out_done, 16 * NT)
            for u in range(XNB):
                sp.wait_ge(xn_out[u], 16 * (NT // XNB))
            for u in range(XB):
                sp.wait_ge(y_out[u], 16 * (ROUTED_TILES // XB))

        @block.gpsimd
        def _(po):
            po.memset(ones_b[:], 1.0)
            po.memset(ones_c[:], 1.0).then_inc(ones_ok, 1)
            po.memset(qkp[:], 0.0).then_inc(pad_ok, 1)
            po.wait_ge(c_in_act, 16 * CONSTS)
            with po.Fori(0, NT) as t:
                po.wait_ge(ln_ok, t + 1)
                po.tensor_tensor(x_all[:, bass.ds(t, 1), :], x_all[:, bass.ds(t, 1), :],
                                 bo_sb[:].unsqueeze(1), ALU.add).then_inc(resid_ok, 1)

            def gather(i, u):
                po.tensor_copy(idx[:, u:u + 1], idx_all[:, bass.ds(i, 1)]).then_inc(idx_col, 1)
                po.wait_ge(idx_col, i + 1)
                po.sem_inc(po_turn, 1)
                po.indirect_dma_start(xg[:, u, :], None, xn_rows[:, :],
                                      bass.IndirectOffsetOnAxis(idx[:, u:u + 1], 0)).then_inc(xg_in[u], 16)

            ROPES = 6

            def rope(t, s, k):
                if not (isinstance(t, int) and t == 0 and k == 0):
                    po.wait_ge(roped, ROPES * t + k)
                    po.sem_inc(po_turn, 1)
                qk = qk_all[:, bass.ds(t, 1), :].rearrange("p o n -> p (o n)")
                v = v_all[:, bass.ds(t, 1), :].rearrange("p o n -> p (o n)")
                q4 = qk.rearrange("p (a h d) -> p a h d", a=2, h=H)
                r4 = rot[:].rearrange("p (a h d) -> p a h d", a=2, h=H)
                if k == 0:
                    i = po.tensor_tensor(qk, qk, bqk_sb[:], ALU.add)
                elif k == 1:
                    i = po.tensor_tensor(r4[:, :, :, 0::2], q4[:, :, :, 1::2], bc_tab(s, 1, 0), ALU.mult)
                elif k == 2:
                    i = po.tensor_tensor(r4[:, :, :, 1::2], q4[:, :, :, 0::2], bc_tab(s, 1, 1), ALU.mult)
                elif k == 3:
                    i = po.tensor_tensor(q4, q4, bc_tab(s, 0, None), ALU.mult)
                elif k == 4:
                    i = po.tensor_tensor(qk, qk, rot[:], ALU.add)
                else:
                    i = po.tensor_tensor(v, v, bv_sb[:], ALU.add)
                i.then_inc(roped, 1)

            per_block = TILES // NT
            assert per_block == 2 * ROPES

            def two_blocks(jj):
                for q in range(2 * per_block):
                    u = q % XB
                    if not (isinstance(jj, int) and jj == 0 and q < XB):
                        po.wait_ge(xt_done, 2 * per_block * jj + q - XB + 1)
                    if isinstance(jj, int) and 2 * per_block * jj + q == SHARED_TILES:
                        po.wait_ge(idx_ok, 2)
                    gather(2 * per_block * jj + q, u)
                    if q % 2:
                        b, k = q // per_block, q % per_block // 2
                        if isinstance(jj, int) and jj == 0 and k == 0:
                            po.wait_ge(qkv_ok, b + 1)
                        rope(2 * jj + b, b, k)

            po.wait_ge(idx_ok, 1)
            for u in range(XNB):
                po.wait_ge(xn_out[u], 16 * (NT // XNB))
            two_blocks(0)
            po.wait_ge(qkv_ok, NT)
            two_blocks(1)
            with po.Fori(2, NT // 2) as jj:
                two_blocks(jj)

            def pads(b, u):
                for s in range(SB):
                    t = SB * b + s
                    qk = qk_all[:, bass.ds(t, 1), :].rearrange("p o n -> p (o n)")
                    q, k = (qk[:, a * E:(a + 1) * E].rearrange("p (h d) -> p h d", d=D) for a in range(2))
                    part = qkp[:, u, s].rearrange("p a h (x d) -> p a h x d", x=2)
                    high = part.bitcast(F32R)

                    def split_step(n):
                        if not (isinstance(t, int) and t == 0 and n == 0):
                            po.wait_ge(padded, SPLITS * t + n)
                            po.sem_inc(po_turn, 1)

                    split_step(0)
                    po.tensor_copy(high[:, 0, :, 0], q)
                    po.tensor_copy(high[:, 0, :, 1], q)
                    po.tensor_copy(high[:, 2, :, 0], k).then_inc(padded, 1)
                    split_step(1)
                    po.tensor_tensor(part[:, 2, :, 1], k, part[:, 2, :, 0], ALU.subtract)
                    po.tensor_tensor(part[:, 1, :, 0], q, part[:, 0, :, 0], ALU.subtract).then_inc(padded, 1)
                    split_step(2)
                    po.tensor_copy(part[:, 1, :, 1], part[:, 1, :, 0]).then_inc(padded, 1)
                    po.wait_ge(padded, SPLITS * (t + 1))
                    po.sem_inc(qkp_ok, 1)

            def rows(t, u):
                po.tensor_copy(cidx[:, u, :], slot_i[:, bass.ds(t, 1), 0:TOPK].rearrange("p o k -> p (o k)")
                               ).then_inc(cidx_ok, 1)
                po.wait_ge(cidx_ok, t + 1)
                po.sem_inc(po_turn, 1)
                for k in range(TOPK):
                    po.indirect_dma_start(yg[u][:, k, :], None, y_rows[:, :],
                                          bass.IndirectOffsetOnAxis(cidx[:, u, k:k + 1], 0)).then_inc(yg_in[u], 16)

            po.wait_ge(roped, ROPES * NT)
            po.wait_ge(pad_ok, 1)
            for b in range(2):
                pads(b, b)
            for s in range(XB):
                po.wait_ge(y_out[s], 16 * (ROUTED_TILES // XB))
            for u in range(2):
                rows(u, u)
            with po.Fori(1, B // 2) as j:
                b = 2 * j
                for u in range(2):
                    po.wait_ge(tq_ok, NR * (b + u) - NR)
                    pads(b + u, u)
                    for s in range(SB):
                        po.wait_ge(dcomb, TOPK * (SB * (b + u - 2) + s + 1))
                        rows(SB * (b + u - 1) + s, s)
            for s in range(SB):
                po.wait_ge(dcomb, TOPK * (SB * (B - 2) + s + 1))
                rows(SB * (B - 1) + s, s)

        @block.scalar
        def _(act):
            act.dma_start(id_f[:], ident).then_inc(c_in_act, 16)
            act.dma_start(bqk_sb[:], bqk.to_broadcast([P, QK])).then_inc(c_in_act, 16)
            act.dma_start(bv_sb[:], bv.to_broadcast([P, E])).then_inc(c_in_act, 16)
            act.dma_start(bo_sb[:], bo.to_broadcast([P, E])).then_inc(c_in_act, 16)
            act.dma_start(rope_sb[:], rope).then_inc(c_in_act, 16)
            act.dma_start(tri_f[:], tri).then_inc(c_in_act, 16)
            act.dma_start(mask_f[:], mask).then_inc(c_in_act, 16)
            act.dma_start(tok_sb[:], tok).then_inc(c_in_act, 16)
            act.dma_start(iota_f[:], iota).then_inc(c_in_act, 16)
            act.wait_ge(var_ok, 1)
            act.activation(rstd[:], var[:], ACT.Sqrt).then_inc(root_ok, 1)
            def xnT_copy(t):
                act.wait_ge(xt_ok, t + 1)
                act.activation(xnT[:, t], bank[t % 2][:, 0:E].rearrange("p (c t) -> p c t", c=EC),
                               ACT.Copy).then_inc(xnT_ok, 1)

            def logits(t):
                act.wait_ge(router_ok, t + 1)
                act.activation(prob[:, t], bank[2 + t % 2][:, 0:NE], ACT.Copy).then_inc(logit_ok, 1)

            for t in range(NT + 1):
                if t < NT:
                    xnT_copy(t)
                if t:
                    logits(t - 1)
            act.wait_ge(exp_in, 1)
            act.activation(prob[:], prob[:], ACT.Exp).then_inc(exp_ok, 1)
            for t in range(NT):
                act.wait_ge(proj_ok, t + 1)
                act.activation(qk_all[:, t], pair[t % 2][:, 0:QK], ACT.Copy)
                act.activation(v_all[:, t], pair[t % 2][:, QK:QK + E], ACT.Copy).then_inc(qkv_ok, 1)

            def clear(u, g0, g1):
                if u == 0:
                    act.wait_ge(dpair, PAIRS * (TOPK + 1))
                act.activation(kT[:, u, g0:g1].rearrange("p g h s -> p (g h s)"),
                               run_b[:, 0, 0:1].to_broadcast([P, (g1 - g0) * G * S]), ACT.Copy).then_inc(kT_clear, 1)

            clear(1, 0, NG)

            def xgT_copy(i, u, shared):
                act.wait_ge(xt_done, i + 1)
                if not (isinstance(i, int) and i < 2):
                    act.wait_ge(gu_ok, i - 1)
                act.activation(xgT[:, u % 2], bank[u % 2][:, 0:E].rearrange("p (c t) -> p c t", c=EC),
                               ACT.Copy).then_inc(xgT_ok, 1)

            def silu(i, u, shared):
                act.wait_ge(gu_ok, i + 1)
                if not (isinstance(i, int) and i < 2):
                    act.wait_ge(hid_ok, i - 1)
                act.activation(sg[:, u % 2], pair[u % 2][:, 0:F], ACT.Silu).then_inc(silu_ok, 1)

            def y_copy(i, u, shared):
                if shared:
                    return
                r = i - SHARED_TILES
                act.wait_ge(dn_ok, i + 1)
                if not (isinstance(i, int) and r < XB):
                    act.wait_ge(y_out[u], 16 // XB * (r - u))
                act.activation(y[:, u], pair[u % 2][:, 512:512 + E], ACT.Copy).then_inc(y_ok, 1)
                act.wait_ge(y_ok, r + 1)
                act.dma_start(y_rows[bass.ds(r * P, P), :], y[:, u]).then_inc(y_out[u], 16)

            def hT_copy(i, u, shared):
                act.wait_ge(at_ok, i + 1)
                if not (isinstance(i, int) and i < 2):
                    act.wait_ge(dn_ok, i - 1)
                act.activation(hT[:, u % 2], bank[2 + u % 2][0:FP, 0:2 * P].rearrange("p (c t) -> p c t", c=2),
                               ACT.Copy).then_inc(hT_ok, 1)

            def ending(u):
                clear(0, u, u + 1)
                if u == XB - 2:
                    act.activation(col[:, 0:1], run_b[:, 0, 0:1], ACT.Exp)

            experts(act, [(3, xgT_copy), (2, silu), (1, hT_copy), (0, y_copy)], ending=ending)

            def tq_copy(b, u, r):
                s, what = ROUNDS[r]
                act.wait_ge(tq_ok, NR * b + r + 1)
                src = bank[r % 2][:].rearrange("p (g t) -> p g t", g=NG)
                if what < 2:
                    dst = (qT_lo if what else qT_hi)[:, u, :, s * P:(s + 1) * P]
                    last = act.activation(dst, src, ACT.Copy)
                for h in range(G if what == 2 else 0):
                    own = slice(h * HP, (h + 1) * HP)
                    last = act.activation(kT[own, u, :, h, s * P:(s + 1) * P], src[own], ACT.Copy)
                last.then_inc(tq_taken, 1)

            def exps(m, n, first):
                p, qt, g = n % 2, n // NG, n % NG
                act.wait_ge(max_ok, m + 1)
                if not first:
                    act.wait_ge(pt_ok, 2 * (m - 1))
                for h in range(G):
                    last = act.activation(prb[:, p, h, 0:(qt + 1) * P],
                                          pair[p][:, h * S:h * S + (qt + 1) * P], ACT.Exp,
                                          bias=negm[:, p, h:h + 1], accum_out=rsum[:, qt, g * G + h:g * G + h + 1])
                last.then_inc(exp_done, 1)

            def oT_copy(c, qt):
                act.wait_ge(ot_ok, c + 1)
                act.activation(oT[:, qt], bank[2 + qt][:, E:2 * E].rearrange("p (c t) -> p c t", c=EC),
                               ACT.Copy).then_inc(ot_taken, 1)

            def a_step(b, n, first, last_b):
                u = n // UNITS
                m, n = UNITS * b + n, n % UNITS
                if 1 <= n <= NR and not last_b:
                    tq_copy(b + u + 1, 1 - u, n - 1)
                if not (last_b and n == UNITS - 1):
                    exps(m + 1, (n + 1) % UNITS, first and n == 0)
                if n % NG == 2 and not (first and n == 2):
                    oT_copy(SB * (b + u) + (0 if n == 6 else -1), 0 if n == 6 else 1)

            act.wait_ge(kT_clear, 1 + NG)
            for u in range(XB):
                act.wait_ge(y_out[u], 16 * (ROUTED_TILES // XB))
            for r in range(FIRST_BLOCK):
                tq_copy(0, 0, r)
            exps(0, 0, True)
            for r in range(FIRST_BLOCK, NR):
                tq_copy(0, 0, r)
            attention(act, a_step)
            oT_copy(SB * B - 1, 1)

        @block.vector
        def _(dve):
            links = [0]

            def link(i):
                links[0] += 1
                i.then_inc(dchain, 1)
                dve.wait_ge(dchain, links[0])

            def layernorm(t):
                u = t % XNB
                if t >= XNB:
                    dve.wait_ge(xt_ok, t - XNB + 1)
                    dve.wait_ge(xn_out[u], 16 * (t // XNB))
                dve.tensor_scalar(xn[:, u], x_all[:, t], mv[:, t, 0:1], rstd[:, t:t + 1], ALU.subtract, ALU.mult
                                  ).then_inc(ln_ok, 1)

            for t in range(NT):
                dve.wait_ge(x_in[t // (NT // 4)], 16)
                last = dve.bn_stats(stats[:, t], x_all[:, t])
            link(last)
            for t in range(NT):
                last = dve.bn_aggr(mv[:, t], stats[:, t])
            link(last)
            link(dve.tensor_scalar_add(var[:], mv[:, :, 1], LN_EPS))
            dve.sem_inc(var_ok, 1)
            dve.wait_ge(c_in_act, 16 * CONSTS)
            dve.tensor_copy(id_b[:], id_f[:])
            dve.tensor_copy(tri_b[:], tri_f[:])
            dve.tensor_copy(mask_b[:], mask_f[:])
            dve.tensor_copy(iota_b[:], iota_f[:])
            dve.memset(run_b[:, 0], 0.0).then_inc(consts_b, 1)
            for e in range(SHARED):
                last = dve.tensor_copy(idx_all[:, e * NT:(e + 1) * NT], tok_sb[:])
            last.then_inc(idx_ok, 1)
            dve.wait_ge(root_ok, 1)
            link(dve.reciprocal(rstd[:], rstd[:]))
            link(dve.tensor_tensor(newton[:], rstd[:], rstd[:], ALU.mult))
            link(dve.tensor_tensor(newton[:], newton[:], var[:], ALU.mult))
            link(dve.tensor_scalar(newton[:], newton[:], -0.5, 1.5, ALU.mult, ALU.add))
            link(dve.tensor_tensor(rstd[:], rstd[:], newton[:], ALU.mult))
            for t in range(NT):
                layernorm(t)

            def over_e(a):
                return a.unsqueeze(2).to_broadcast([P, NT, NE])

            dve.wait_ge(logit_ok, NT)
            link(dve.tensor_reduce(col[:], prob[:], AX.X, ALU.max, negate=True))
            dve.tensor_tensor(prob[:], prob[:], over_e(col[:]), ALU.add).then_inc(exp_in, 1)
            dve.wait_ge(exp_ok, 1)
            link(dve.tensor_reduce(col[:], prob[:], AX.X, ALU.add))
            link(dve.reciprocal(col[:], col[:]))
            link(dve.tensor_tensor(prob[:], prob[:], over_e(col[:]), ALU.mult))
            for t in range(NT):
                last = dve.max(top[:, t], prob[:, t])
            link(last)
            link(dve.tensor_reduce(wsum[:], top[:, :, 0:TOPK], AX.X, ALU.add))
            link(dve.tensor_scalar_add(wsum[:], wsum[:], TOP_EPS))
            link(dve.reciprocal(wsum[:], wsum[:]))
            sixth = over_e(top[:, :, TOPK - 1])
            link(dve.tensor_tensor(sel[:], prob[:], sixth, ALU.is_gt))
            link(dve.tensor_reduce(col[:], sel[:], AX.X, ALU.add))
            link(dve.tensor_scalar(col[:], col[:], -1.0, float(TOPK), ALU.mult, ALU.add))
            link(dve.tensor_tensor(tmp[:], prob[:], sixth, ALU.is_equal))
            for t in range(NT):
                last = dve.tensor_tensor_scan(key[:, t], tmp[:, t], tmp[:, t], 0.0, ALU.add, ALU.max)
            link(last)
            link(dve.tensor_tensor(key[:], key[:], over_e(col[:]), ALU.is_le))
            link(dve.tensor_tensor(key[:], key[:], tmp[:], ALU.mult))
            link(dve.tensor_tensor(sel[:], sel[:], key[:], ALU.add))
            link(dve.tensor_tensor(comb[:], prob[:], sel[:], ALU.mult))
            link(dve.tensor_tensor(comb[:], comb[:], over_e(wsum[:]), ALU.mult))
            link(dve.tensor_copy(sel_b[:], sel[:]))
            for t in range(NT):
                link(dve.tensor_tensor(run_b[:, t + 1], run_b[:, t], sel_b[:, t], ALU.add))
            dve.sem_inc(chosen, 1)
            dve.wait_ge(counted, 1)
            link(dve.tensor_copy(cnt[:], bank[2][0:NE, 0:1]))
            dve.wait_ge(c_in, 16 * 5)
            link(dve.tensor_scalar(over[:], thr_sb[:], cnt[:], None, ALU.is_lt))
            link(dve.tensor_reduce(ntile[:], over[:], AX.X, ALU.add))
            dve.tensor_copy(ntile_b[:], ntile[:].to_broadcast([NE, P])).then_inc(tiled, 1)
            dve.wait_ge(placed, 1)
            link(dve.tensor_copy(cend[:], bank[2][0:NE, 1:2]))
            dve.tensor_scalar(passed[:], tileno_sb[:], cend[:], None, ALU.is_ge).then_inc(passed_ok, 1)
            link(dve.tensor_scalar(place[:], bank[3][:, 0:NE], float(P), 1.0, ALU.mult, ALU.add))
            half = NT // 2
            for h in range(2):
                last = dve.tensor_tensor(key[:, half * h:half * (h + 1)], bank[h][:].rearrange("p (t e) -> p t e", e=NE),
                                         place[:].unsqueeze(1).to_broadcast([P, half, NE]), ALU.add)
            link(last)
            link(dve.tensor_tensor(key[:], key[:], sel[:], ALU.mult))
            for t in range(NT):
                last = dve.max(top[:, t], key[:, t])
            link(last)
            link(dve.tensor_scalar_add(slot_f[:], top[:], -1.0))
            link(dve.tensor_copy(slot_i[:], slot_f[:]))
            link(dve.tensor_scalar(part_i[:], slot_i[:], P - 1, None, ALU.bitwise_and))
            link(dve.tensor_copy(slot_row[:], part_i[:]))
            link(dve.tensor_scalar(part_i[:], slot_i[:], SHIFT, None, ALU.arith_shift_right))
            link(dve.tensor_copy(slot_tile[:], part_i[:]))
            for e in range(SHARED):
                dve.memset(tile_ef[:, e * NT:(e + 1) * NT], float(e))
                dve.memset(last_tf[:, e:e + 1], float((e + 1) * NT))
            dve.wait_ge(ended, 1)
            dve.tensor_scalar(tile_ef[:, SHARED_TILES:TILES], bank[2][0:1, 128:128 + ROUTED_TILES], float(SHARED),
                              float(XT - 1), ALU.add, ALU.min)
            link(dve.tensor_scalar_add(last_tf[:, SHARED:XT], bank[2][0:1, 64:64 + NE], float(SHARED_TILES)))
            dve.tensor_copy(tile_e[:], tile_ef[:])
            dve.tensor_copy(last_t[:], last_tf[:]).then_inc(tables_ok, 1)
            def one_hot(q, slots):
                for n in slots:
                    u, k = n // TOPK, n % TOPK
                    t = 2 * q + u
                    dve.tensor_scalar(is_row[:, u, k], iota_b[:, 0:P],
                                      slot_row[:, bass.ds(t, 1), k:k + 1].rearrange("p o k -> p (o k)"),
                                      None, ALU.is_equal)
                    last_k = dve.tensor_scalar(is_tile[:, u, k], iota_b[:],
                                               slot_tile[:, bass.ds(t, 1), k:k + 1].rearrange("p o k -> p (o k)"),
                                               tok_sb[:, bass.ds(t, 1)], ALU.is_equal, ALU.mult)
                return last_k

            def take(pair_no):
                dve.wait_ge(listed, pair_no + 1)
                part = bank[0][:, E:E + ROUTED_TILES]
                if isinstance(pair_no, int) and pair_no == 0:
                    dve.tensor_copy(token_no[:], part).then_inc(list_taken, 1)
                else:
                    dve.wait_ge(list_taken, pair_no)
                    dve.tensor_tensor(token_no[:], token_no[:], part, ALU.add).then_inc(list_taken, 1)

            for q in range(EARLY):
                one_hot(q, range(2 * TOPK)).then_inc(onehot_ok, 1)
                take(q)

            def list_beside(j, u):
                q = j + EARLY - 1
                part = 2 * TOPK // (XB - 1)
                if u == XB - 1:
                    take(q)
                else:
                    last = one_hot(q, range(part * u, part * (u + 1)))
                    if u == XB - 2:
                        last.then_inc(onehot_ok, 1)

            def listed_all():
                dve.wait_ge(list_taken, NT // 2)
                dve.tensor_copy(idx_all[:, SHARED_TILES:TILES], token_no[:]).then_inc(idx_ok, 1)

            def hidden(i, u, shared):
                dve.wait_ge(silu_ok, i + 1)
                if not (isinstance(i, int) and i < 2):
                    dve.wait_ge(at_ok, i - 1)
                dve.tensor_tensor(hid[:, u % 2], sg[:, u % 2], pair[u % 2][:, F:2 * F], ALU.mult).then_inc(hid_ok, 1)

            def y_add(i, u, shared):
                if not shared:
                    return
                dve.wait_ge(dn_ok, i + 1)
                if not (isinstance(i, int) and i == 0):
                    dve.wait_ge(y_added, i)
                xa = x_all[:, bass.ds(i % NT, 1), :].rearrange("p o e -> p (o e)")
                dve.tensor_tensor(xa, xa, pair[u % 2][:, 512:512 + E], ALU.add).then_inc(y_added, 1)

            def slot_weights(j):
                k = j - W6_TURN
                dve.tensor_tensor(tmp[:], key[:], top[:, :, bass.ds(k, 1)].to_broadcast([P, NT, NE]), ALU.is_equal
                                  ).then_inc(dpair, 1)
                dve.wait_ge(dpair, PAIRS * k + 1)
                dve.tensor_tensor(tmp[:], tmp[:], comb[:], ALU.mult).then_inc(dpair, 1)
                dve.wait_ge(dpair, PAIRS * k + 2)
                dve.tensor_reduce(w6[:, :, bass.ds(k, 1)], tmp[:], AX.X, ALU.add).then_inc(dpair, 1)

            dve.wait_ge(resid_ok, NT)
            experts(dve, [(2, hidden), (0, y_add)], list_beside, listed_all, slot_weights)

            def maxes(m, n):
                p, qt = n % 2, n // NG
                dve.wait_ge(s_ok, m + 1)
                dve.tensor_reduce(negm[:, p], pair[p][:].rearrange("p (h k) -> p h k", h=G)[:, :, 0:(qt + 1) * P],
                                  AX.X, ALU.max, negate=True).then_inc(max_ok, 1)

            def pT_copy(m, n):
                p, qt = n % 2, n // NG
                if not (isinstance(m, int) and m < 2):
                    dve.wait_ge(av_ok, m - 1)
                k = 2 * (qt + 1)
                for half in range(2):
                    dve.wait_ge(pt_ok, 2 * m + half + 1)
                    dve.tensor_copy(pT[:, p, k * half:k * (half + 1), :],
                                    bank[half][:, 0:k * P].rearrange("p (k q) -> p k q", k=k)).then_inc(pt_taken, 1)

            def normalise(c, qt):
                dve.wait_ge(av_ok, NG * (c + 1))
                dve.reciprocal(rrec[:, qt], rsum[:, qt]).then_inc(drec, 1)
                dve.wait_ge(drec, c + 1)
                dve.tensor_tensor(on[:, qt].rearrange("p (h d) -> p h d", d=D),
                                  bank[2 + qt][:, 0:E].rearrange("p (h d) -> p h d", d=D),
                                  rrec[:, qt].unsqueeze(2).to_broadcast([P, H, D]), ALU.mult).then_inc(on_ok, 1)

            def residual(c, qt):
                dve.wait_ge(wo_ok, c + 1)
                dve.wait_ge(dcomb, TOPK * (c + 1))
                xa = x_all[:, bass.ds(c, 1), :].rearrange("p o e -> p (o e)")
                dve.tensor_tensor(xa, xa, bank[2 + qt][:, 0:E], ALU.add).then_inc(res_ok, 1)

            def combine(t, u, slots):
                dve.wait_ge(yg_in[u], 16 * TOPK * (t // 2 + 1) if isinstance(t, int) else 8 * TOPK * (t - u) + 16 * TOPK)
                xa = x_all[:, bass.ds(t, 1), :].rearrange("p o e -> p (o e)")
                for k in slots:
                    if not (isinstance(t, int) and t == 0 and k == 0):
                        dve.wait_ge(dcomb, TOPK * t + k)
                    w = w6[:, bass.ds(t, 1), k:k + 1].rearrange("p o k -> p (o k)")
                    dve.scalar_tensor_tensor(xa, yg[u][:, k], w, xa, ALU.mult, ALU.add).then_inc(dcomb, 1)

            def d_step(b, n, first, last_b):
                u = n // UNITS
                m, n = UNITS * b + n, n % UNITS
                if not (last_b and n == UNITS - 1):
                    maxes(m + 1, (n + 1) % UNITS)
                pT_copy(m, n)
                if n % NG:
                    combine(SB * (b + u) + n // NG, n // NG, range(2 * (n % NG) - 2, 2 * (n % NG)))
                if n % NG == 0 and not (first and n == 0):
                    normalise(SB * (b + u) + (0 if n else -1), 0 if n else 1)
                if n % NG == 3 and not (first and n == 3):
                    residual(SB * (b + u) + (0 if n == 7 else -1), 0 if n == 7 else 1)

            dve.wait_ge(y_added, SHARED_TILES)
            dve.wait_ge(dpair, PAIRS * (TOPK + 1))
            maxes(0, 0)
            attention(dve, d_step)
            normalise(SB * B - 1, 1)
            residual(SB * B - 1, 1)

        @block.tensor
        def _(pe):
            pe.wait_ge(c_in_act, 16 * CONSTS)
            pe.wait_ge(consts_b, 1)

            def xn_transpose(t):
                pe.wait_ge(ln_ok, t + 1)
                if t >= 2:
                    pe.wait_ge(xnT_ok, t - 1)
                for c in range(EC):
                    last = pe.transpose(bank[t % 2][:, c * P:(c + 1) * P], xn[:, t % XNB, c * P:(c + 1) * P], id_f[:])
                last.then_inc(xt_ok, 1)

            def route(t):
                pe.wait_ge(xnT_ok, t + 1)
                if t >= 2:
                    pe.wait_ge(logit_ok, t - 1)
                for c in range(EC):
                    last = pe.matmul(bank[2 + t % 2][:, 0:NE], xnT[:, t, c], wr_sb[:, c], start=c == 0, stop=c == EC - 1)
                last.then_inc(router_ok, 1)

            pe.wait_ge(wr_in, 16)
            for t in range(NT + 1):
                if t < NT:
                    xn_transpose(t)
                if t:
                    route(t - 1)

            def project(t):
                if t >= 2:
                    pe.wait_ge(qkv_ok, t - 1)
                for n0, n1 in ((0, QK), (QK, QK + E)):
                    for c in range(EC):
                        last = pe.matmul(pair[t % 2][:, n0:n1], xnT[:, t, c], wqkv_sb[:, c, n0:n1],
                                         start=c == 0, stop=c == EC - 1)
                last.then_inc(proj_ok, 1)

            pe.wait_ge(w_in, 16)
            at_plan, pause = NT - 2 * (NT // 5), NT // 5
            for t in range(at_plan):
                project(t)

            pe.wait_ge(chosen, 1)
            pe.wait_ge(ones_ok, 1)
            for h in range(2):
                o = bank[h][:]
                t0, t1 = NT // 2 * h, NT // 2 * (h + 1)
                pe.matmul(o, tri_b[:], sel_b[:, t0:t1].rearrange("p t e -> p (t e)"), start=True, stop=False)
                pe.matmul(o, ones_b[:], run_b[:, t0:t1].rearrange("p t e -> p (t e)"), start=False, stop=True)
            pe.matmul(bank[2][0:NE, 0:1], run_b[:, NT], ones_b[:, 0:1], start=True, stop=True).then_inc(counted, 1)
            pe.wait_ge(tiled, 1)
            pe.matmul(bank[3][:, 0:NE], ntile_b[:], before_sb[:], start=True, stop=True)
            pe.matmul(bank[2][0:NE, 1:2], upto_sb[:], ntile[:], start=True, stop=True)
            pe.matmul(bank[2][0:1, 64:64 + NE], ntile[:], upto_sb[:], start=True, stop=True).then_inc(placed, 1)
            pe.wait_ge(passed_ok, 1)
            pe.matmul(bank[2][0:1, 128:128 + ROUTED_TILES], ones_c[:], passed[:], start=True, stop=True
                      ).then_inc(ended, 1)
            pe.wait_ge(tables_ok, 1)

            def list_tokens(pair_no):
                pe.wait_ge(onehot_ok, pair_no + 1)
                for u in range(2):
                    for k in range(TOPK):
                        mm = pe.matmul(bank[0][:, E:E + ROUTED_TILES], is_row[:, u, k], is_tile[:, u, k],
                                       start=u == 0 and k == 0, stop=u == 1 and k == TOPK - 1)
                mm.then_inc(listed, 1)

            for q in range(EARLY):
                for t in range(at_plan + pause * q, at_plan + pause * (q + 1)):
                    project(t)
                if q:
                    pe.wait_ge(list_taken, q)
                list_tokens(q)
            pe.wait_ge(qkv_ok, NT)
            pe.wait_ge(list_taken, EARLY)

            def list_beside(j, u):
                if u == XB - 1:
                    pe.wait_ge(xgT_ok, XB * j + u + 3 + 1)
                    list_tokens(j + EARLY - 1)

            expert_reg = [pe.alloc_register(f"expert{u}") for u in range(XB)]

            def load_expert(i, u):
                pe.reg_load(expert_reg[u], tile_e[0:1, bass.ds(i, 1)])

            def expert_of(u):
                return pe.snap(expert_reg[u], min_val=0, max_val=XT - 1) & (P - 1)

            def x_transpose(i, u, shared):
                pe.wait_ge(xg_in[u], 16 * (i // XB + 1) if isinstance(i, int) else (i - u) * 4 + 16)
                if not (isinstance(i, int) and i < 2):
                    pe.wait_ge(xgT_ok, i - 1)
                if u == 0 and (i == SHARED_TILES if isinstance(i, int) else shared):
                    pe.wait_ge(list_taken, i // XB + EARLY - 2)
                for c in range(EC):
                    last = pe.transpose(bank[u % 2][:, c * P:(c + 1) * P], xg[:, u, c * P:(c + 1) * P], id_f[:])
                last.then_inc(xt_done, 1)

            def up(i, u, shared):
                e = expert_of(u)
                pe.wait_ge(xgT_ok, i + 1)
                if not (isinstance(i, int) and i < 2):
                    pe.wait_ge(hid_ok, i - 1)
                pe.wait_ge(w_ready, e + 1)
                for c in range(EC):
                    w = wgu_sb[:, bass.ds(e % WB, 1), c, :].rearrange("p o n -> p (o n)")
                    last = pe.matmul(pair[u % 2][:, 0:2 * F], xgT[:, u % 2, c], w, start=c == 0, stop=c == EC - 1)
                last.then_inc(gu_ok, 1)
                if not (isinstance(i, int) and i + 1 >= TILES):
                    load_expert(i + 1, (u + 1) % XB)

            def h_transpose(i, u, shared):
                pe.wait_ge(hid_ok, i + 1)
                if not (isinstance(i, int) and i < 2):
                    pe.wait_ge(hT_ok, i - 1)
                for c in range(2):
                    last = pe.transpose(bank[2 + u % 2][0:FP, c * P:(c + 1) * P], hid[:, u % 2, c * FP:(c + 1) * FP],
                                        id_f[:])
                last.then_inc(at_ok, 1)

            def down(i, u, shared):
                e = expert_of(u)
                pe.wait_ge(hT_ok, i + 1)
                if shared or isinstance(i, int) and i < SHARED_TILES + 2:
                    if not (isinstance(i, int) and i < 2):
                        pe.wait_ge(y_added, i - 1)
                else:
                    pe.wait_ge(y_ok, i - SHARED_TILES - 1)
                for c in range(2):
                    w = wdn_sb[:, bass.ds(e % WB, 1), c, :].rearrange("p o n -> p (o n)")
                    last = pe.matmul(pair[u % 2][:, 512:512 + E], hT[:, u % 2, c], w, start=c == 0, stop=c == 1)
                last.then_inc(dn_ok, 1)

            load_expert(0, 0)
            experts(pe, [(3, x_transpose), (2, up), (1, h_transpose), (0, down)], list_beside)

            def tq(b, u, r, m):
                s, what = ROUNDS[r]
                if r == 0:
                    pe.wait_ge(qkp_ok, SB * (b + 1))
                if m is not None:
                    pe.wait_ge(pt_taken, 2 * (m - 1) + 1 + r % 2)
                elif r >= 2:
                    pe.wait_ge(tq_taken, r - 1)
                for g in range(NG):
                    last = pe.transpose(bank[r % 2][:, g * P:(g + 1) * P],
                                        qkp[:, u, s, what, g * G:(g + 1) * G, :].rearrange("p h d -> p (h d)"), id_f[:])
                last.then_inc(tq_ok, 1)

            def scores(m, n, b, u, first):
                p, qt, g = n % 2, n // NG, n % NG
                if g == 0:
                    pe.wait_ge(tq_taken, NR * (b + 1) if qt else NR * b + FIRST_BLOCK)
                if not first:
                    pe.wait_ge(exp_done, m - 1)
                for h in range(G):
                    o = pair[p][:, h * S:(h + 1) * S]
                    for i, q in enumerate((qT_hi, qT_lo)):
                        pe.matmul(o[:, 0:(qt + 1) * P], q[:, u, g, qt * P:(qt + 1) * P],
                                  kT[:, u, g, h, 0:(qt + 1) * P], start=i == 0, stop=False)
                    last = pe.matmul(o[:, qt * P:(qt + 1) * P], id_b[:], mask_b[:], start=False, stop=True)
                last.then_inc(s_ok, 1)

            def p_transpose(m, n, tq_round):
                p, qt = n % 2, n // NG
                pe.wait_ge(exp_done, m + 1)
                for half in range(2):
                    if not (isinstance(m, int) and m < 1):
                        pe.wait_ge(pt_taken, 2 * (m - 1) + half + 1)
                    if tq_round is not None and half == tq_round[1] % 2:
                        pe.wait_ge(tq_taken, NR * tq_round[0] + tq_round[1] + 1)
                    i = 0
                    for h in range(2 * half, 2 * half + 2):
                        for kb in range(qt + 1):
                            last = pe.transpose(bank[half][:, i * P:(i + 1) * P],
                                                prb[:, p, h, kb * P:(kb + 1) * P], id_f[:])
                            i += 1
                    last.then_inc(pt_ok, 1)

            def values(m, n, b, first2):
                p, qt, g = n % 2, n // NG, n % NG
                pe.wait_ge(pt_taken, 2 * m + 2)
                if g == 0 and not first2:
                    pe.wait_ge(res_ok, SB * b + qt - 1)
                for h in range(G):
                    o = (g * G + h) * D
                    for kb in range(qt + 1):
                        vb = v_all[:, bass.ds(SB * b + kb, 1), o:o + D].rearrange("p o d -> p (o d)")
                        last = pe.matmul(bank[2 + qt][:, o:o + D], pT[:, p, h * (qt + 1) + kb, :], vb,
                                         start=kb == 0, stop=kb == qt)
                last.then_inc(av_ok, 1)

            def o_transpose(c, qt):
                pe.wait_ge(on_ok, c + 1)
                for k in range(EC):
                    last = pe.transpose(bank[2 + qt][:, E + k * P:E + (k + 1) * P], on[:, qt, k * P:(k + 1) * P], id_f[:])
                last.then_inc(ot_ok, 1)

            def o_project(c, qt):
                pe.wait_ge(ot_taken, c + 1)
                for k in range(EC):
                    last = pe.matmul(bank[2 + qt][:, 0:E], oT[:, qt, k], wo_sb[:, k], start=k == 0, stop=k == EC - 1)
                last.then_inc(wo_ok, 1)

            def p_step(b, n, first, last_b):
                u = n // UNITS
                m, n, bb = UNITS * b + n, n % UNITS, b + u
                if not (last_b and n == UNITS - 1):
                    nu = 1 - u if n == UNITS - 1 else u
                    scores(m + 1, (n + 1) % UNITS, bb + (1 if n == UNITS - 1 else 0), nu, first and n == 0)
                rnd = None
                if 1 <= n <= NR and not last_b:
                    rnd = (bb + 1, n - 1)
                    tq(bb + 1, 1 - u, n - 1, m)
                if not (first and n == 0):
                    values(m - 1, (n - 1) % UNITS, bb - (1 if n == 0 else 0), first)
                if n % NG == 2 and not (first and n == 2):
                    o_transpose(SB * bb + (0 if n == 6 else -1), 0 if n == 6 else 1)
                p_transpose(m, n, rnd)
                if n % NG == 3 and not (first and n == 3):
                    o_project(SB * bb + (0 if n == 7 else -1), 0 if n == 7 else 1)

            pe.wait_ge(y_ok, ROUTED_TILES)
            for r in range(FIRST_BLOCK):
                tq(0, 0, r, None)
            scores(0, 0, 0, 0, True)
            for r in range(FIRST_BLOCK, NR):
                tq(0, 0, r, None)
            pe.wait_ge(tq_taken, NR)
            attention(pe, p_step)
            values(UNITS * B - 1, UNITS - 1, B - 1, False)
            o_transpose(SB * B - 1, 1)
            o_project(SB * B - 1, 1)
            pe.wait_ge(res_ok, SB * B)


def _tables():
    import numpy as np
    pos = np.arange(S, dtype=np.float32)[:, None]
    exps = -np.arange(0, D, 2, dtype=np.float32) / np.float32(D)
    theta = np.repeat(np.power(np.float32(10000.0), exps), 2)
    angle = pos * theta[None, :]
    cos, sin = np.cos(angle), np.sin(angle)
    sin[:, 0::2] *= -1.0
    rope = np.stack([cos, sin], 1)[:, :, None, :] * np.array([D ** -0.5, 1.0], np.float32)[None, None, :, None]
    r, c = np.arange(P)[:, None], np.arange(P)[None, :]
    e = np.arange(NE)
    f = np.float32
    return {
        "rope": rope.reshape(SB, P, 2, 2, D).transpose(1, 0, 2, 3, 4).astype(f).copy(),
        "tri": (r < c).astype(f), "ident": (r == c).astype(f), "mask": np.where(c > r, MASKED, 0.0).astype(f),
        "before": (e[:, None] < e[None, :]).astype(f), "upto": (e[:, None] <= e[None, :]).astype(f),
        "tileno": np.tile(np.arange(ROUTED_TILES, dtype=f), (NE, 1)),
        "thr": np.tile(P * np.arange(NT, dtype=f), (NE, 1)),
        "iota": np.tile(np.arange(ROUTED_TILES, dtype=f), (P, 1)),
        "tok": (np.arange(NT)[None, :] * P + np.arange(P)[:, None]).astype(f),
    }


def kernel(**inputs):
    import numpy as np
    import concourse.bacc as bacc
    from concourse.bass_utils import run_bass_kernel_spmd

    a = {k: np.asarray(v) for k, v in inputs.items()}
    sgu = a["L0_ffn_ws_gate_up"].reshape(2, SHARED, F, E).transpose(1, 0, 2, 3).reshape(SHARED, 2 * F, E)
    sdn = a["L0_ffn_ws_down"].reshape(E, SHARED, F).transpose(1, 0, 2)
    gu = np.concatenate([sgu, a["L0_ffn_w_gate_up"]], 0)
    dn = np.concatenate([sdn, a["L0_ffn_w_down"]], 0)
    arrays = {
        "x": a["L0_attn_x"].reshape(T, E),
        "wqkv": np.concatenate([a["L0_attn_Wq"], a["L0_attn_Wk"], a["L0_attn_Wv"]], 1),
        "bqk": np.concatenate([a["L0_attn_bq"], a["L0_attn_bk"]])[None, :],
        "bv": a["L0_attn_bv"][None, :], "bo": a["L0_attn_bo"][None, :], "wo": a["L0_attn_Wo"],
        "wr": a["L0_ffn_gate_w"].T,
        "wgu": gu.transpose(0, 2, 1).reshape(XT, EC, P, 2 * F).transpose(0, 2, 1, 3).reshape(XT, P, EC * 2 * F),
        "wdn": dn.transpose(0, 2, 1).reshape(XT, 2, FP, E).transpose(0, 2, 1, 3).reshape(XT, FP, 2 * E),
    }
    arrays.update(_tables())
    arrays = {k: np.ascontiguousarray(v) for k, v in arrays.items()}
    nc = bacc.Bacc("TRN2", target_bir_lowering=False, num_devices=1)
    args = {k: nc.dram_tensor(k, v.shape, mybir.dt.from_np(v.dtype), kind="ExternalInput").ap()
            for k, v in arrays.items()}
    out = nc.dram_tensor("out", (T, E), F32, kind="ExternalOutput").ap()
    build(nc, *[args[k] for k in ("x", "wqkv", "bqk", "bv", "bo", "wo", "wr", "wgu", "wdn", "rope", "tri", "ident",
                                  "mask", "before", "upto", "tileno", "thr", "tok", "iota")], out)
    r = run_bass_kernel_spmd(nc, [arrays], core_ids=[0])
    return r.results[0]["out"].reshape(B, S, E)
```
